# Optimizing a Trainium2 kernel written in Bass

```python
import numpy as np
import jax
import jax.numpy as jnp

def _softmax(x, axis=-1):
    return jax.nn.softmax(x, axis=axis)
def _gelu(x):
    return jax.nn.gelu(x, approximate=True)
def _silu(x):
    return jax.nn.silu(x)
def _sigmoid(x):
    return jax.nn.sigmoid(x)
def _layernorm(x, axis=-1, eps=1e-5):
    m = jnp.mean(x, axis=axis, keepdims=True)
    v = jnp.var(x, axis=axis, keepdims=True)
    return (x - m) / jnp.sqrt(v + eps)
def _scatter_add(tgt, idx, src, axis=0):
    return tgt.at[idx].add(src)
def _segment_sum(src, seg, n):
    return jax.ops.segment_sum(src, seg, n)

kernel_name = 'mk_conv_seq_d1_conv_nchw512_d5b107'

def setup_inputs(seed: int = 0):
    np.random.seed(seed)
    _w = jnp.asarray
    def _rec_inputs():
        import jax
        import jax.numpy as jnp
        _gk = jax.random.key(seed)
        x = 7.22e-05 + 1 * jax.random.normal(jax.random.fold_in(_gk, 1), (16, 512, 32, 32), jnp.float32)
        return x
    x = _rec_inputs()
    def _L0_conv_setup():
        import jax, jax.numpy as jnp
        import numpy as np
        NUM_HEADS = 8
        NUM_GROUPS = 32
        EPS = 1e-05

        def group_norm(x, scale, bias):
            b, c, t = x.shape
            xg = x.reshape(b, NUM_GROUPS, c // NUM_GROUPS, t)
            mean = xg.mean(axis=(2, 3), keepdims=True)
            var = xg.var(axis=(2, 3), keepdims=True)
            xn = ((xg - mean) * jax.lax.rsqrt(var + EPS)).reshape(b, c, t)
            return xn * scale[None, :, None] + bias[None, :, None]
        key = jax.random.key(seed)
        ks = jax.random.split(key, 3)
        b, c, h, w = (16, 512, 32, 32)
        x = jax.random.normal(ks[0], (b, c, h, w), dtype=jnp.float32)
        gn_scale = jnp.ones((c,), jnp.float32)
        gn_bias = jnp.zeros((c,), jnp.float32)
        w_qkv = jax.random.normal(ks[1], (3 * c, c), jnp.float32) * c ** (-0.5)
        b_qkv = jnp.zeros((3 * c,), jnp.float32)
        w_proj = jax.random.normal(ks[2], (c, c), jnp.float32) * c ** (-0.5)
        b_proj = jnp.zeros((c,), jnp.float32)
        return {'x': x, 'gn_scale': gn_scale, 'gn_bias': gn_bias, 'w_qkv': w_qkv, 'b_qkv': b_qkv, 'w_proj': w_proj, 'b_proj': b_proj}
    _L0_conv_all = _L0_conv_setup()
    _L0_conv_in = {k: v for k, v in _L0_conv_all.items() if k in ('gn_scale', 'gn_bias', 'w_qkv', 'b_qkv', 'w_proj', 'b_proj', )}
    del _L0_conv_all

    return {
        "x": x,
        "L0_conv_gn_scale": _L0_conv_in["gn_scale"],
        "L0_conv_gn_bias": _L0_conv_in["gn_bias"],
        "L0_conv_w_qkv": _L0_conv_in["w_qkv"],
        "L0_conv_b_qkv": _L0_conv_in["b_qkv"],
        "L0_conv_w_proj": _L0_conv_in["w_proj"],
        "L0_conv_b_proj": _L0_conv_in["b_proj"],
    }

def reference(x, L0_conv_gn_scale, L0_conv_gn_bias, L0_conv_w_qkv, L0_conv_b_qkv, L0_conv_w_proj, L0_conv_b_proj):
    import jax
    import jax.numpy as jnp
    def _L0_conv_ref(x, gn_scale, gn_bias, w_qkv, b_qkv, w_proj, b_proj):
        import jax, jax.numpy as jnp
        import numpy as np
        NUM_HEADS = 8
        NUM_GROUPS = 32
        EPS = 1e-05

        def group_norm(x, scale, bias):
            b, c, t = x.shape
            xg = x.reshape(b, NUM_GROUPS, c // NUM_GROUPS, t)
            mean = xg.mean(axis=(2, 3), keepdims=True)
            var = xg.var(axis=(2, 3), keepdims=True)
            xn = ((xg - mean) * jax.lax.rsqrt(var + EPS)).reshape(b, c, t)
            return xn * scale[None, :, None] + bias[None, :, None]
        b, c, h, w = x.shape
        t = h * w
        xf = x.reshape(b, c, t)
        xn = group_norm(xf, gn_scale, gn_bias)
        qkv = jnp.einsum('oc,bct->bot', w_qkv, xn) + b_qkv[None, :, None]
        dh = c // NUM_HEADS
        qkv = qkv.reshape(b * NUM_HEADS, 3 * dh, t)
        q, k, v = jnp.split(qkv, 3, axis=1)
        scale = dh ** (-0.25)
        logits = jnp.einsum('bct,bcs->bts', q * scale, k * scale)
        weight = jax.nn.softmax(logits.astype(jnp.float32), axis=-1).astype(logits.dtype)
        attn = jnp.einsum('bts,bcs->bct', weight, v)
        attn = attn.reshape(b, c, t)
        out = jnp.einsum('oc,bct->bot', w_proj, attn) + b_proj[None, :, None]
        return (xf + out).reshape(b, c, h, w)

    def _gn(v, G=32, eps=1e-5):
        B_, C_, H_, W_ = v.shape
        g = v.reshape(B_, G, C_ // G, H_, W_)
        m = jnp.mean(g, axis=(2, 3, 4), keepdims=True)
        s = jnp.var(g, axis=(2, 3, 4), keepdims=True)
        return ((g - m) / jnp.sqrt(s + eps)).reshape(v.shape)

    def _ln_c(v, eps=1e-6):
        m = jnp.mean(v, axis=1, keepdims=True)
        s = jnp.var(v, axis=1, keepdims=True)
        return (v - m) / jnp.sqrt(s + eps)

    def _ln_t(v, eps=1e-5):
        m = jnp.mean(v, axis=-1, keepdims=True)
        s = jnp.var(v, axis=-1, keepdims=True)
        return (v - m) / jnp.sqrt(s + eps)

    def _to_tokens(v):
        B_, C_, H_, W_ = v.shape
        return v.reshape(B_, C_, H_ * W_).transpose(0, 2, 1)
    def _from_tokens(t, like):
        B_, C_, H_, W_ = like.shape
        return t.transpose(0, 2, 1).reshape(B_, C_, H_, W_)

    x = _L0_conv_ref(x, L0_conv_gn_scale, L0_conv_gn_bias, L0_conv_w_qkv, L0_conv_b_qkv, L0_conv_w_proj, L0_conv_b_proj)
    return x


_drawn_inputs = setup_inputs


def setup_inputs(seed=0):
    import zlib

    import numpy as np

    out = dict(_drawn_inputs(seed))
    spreads = {'L0_conv_gn_scale': (1.0, 0.545),
     'L0_conv_gn_bias': (0.0, 0.1),
     'L0_conv_b_qkv': (0.0, 0.1),
     'L0_conv_b_proj': (0.0, 0.1)}
    factors = {}
    for name, (base, spread) in spreads.items():
        noise = np.random.default_rng([zlib.crc32(name.encode()), seed]).standard_normal(out[name].shape)
        drawn = base * np.exp(spread * noise) if base else spread * noise
        out[name] = jnp.asarray(drawn.astype(out[name].dtype))
    for name, factor in factors.items():
        out[name] = (out[name] * factor).astype(out[name].dtype)
    return out
```

```python
from contextlib import ExitStack

import concourse.bass as bass
from concourse import mybir

F32 = mybir.dt.float32
F32R = mybir.dt.float32r
F16 = mybir.dt.float16
ALU = mybir.AluOpType
ACT = mybir.ActivationFunctionType
AX = mybir.AxisListType

B, C, T = 16, 512, 1024
HEADS, DH = 8, 64
GROUPS, EPS = 32, 1e-5
P = 128
KT = C // P
PAIRS = HEADS // 2
ITERS = B * PAIRS
NS = T // P
HALF = 512
QK_SCALE = float(DH) ** -0.25
XN_MAX = 128.0
V_RANGE = 32768.0
P_SHIFT = 4 * 0.6931471805599453
VW = 2 * DH + 2
OT_BANK = 3

PL_ON_DVE = (2, 7)


def slots_of(i_static, x, tail, prep, xprep):
    y = 1 - x
    slots = [[] for _ in range(NS)]
    if prep:
        slots[0] += [("qk", y, 0)]
        slots[1] += [("qk", y, 1)]
        for k in range(4):
            slots[3 + k] += [("max", y, tt, u) for tt in (2 * k, 2 * k + 1) for u in (0, 1)]
        slots[7] += [("m", y)]
    if x == 0:
        if xprep:
            slots[1] += [("mean",)]
            slots[2] += [("var",)]
        slots[2] += [("vt", 1)]
        if tail:
            slots[3] += [("ot", 0)]
            slots[4] += [("ot", 1)]
            slots[6] += [("proj", 0)]
            slots[7] += [("proj", 1), ("proj", 2), ("proj", 3)]
    else:
        if tail:
            slots[0] += [("proj", 4)]
            slots[1] += [("proj", 5)]
        if prep:
            slots[2] += [("v", 0)]
            slots[3] += [("v", 1)]
            slots[4] += [("vt", 0)]
        if tail:
            slots[5] += [("proj", 6)]
            slots[6] += [("proj", 7)]
    return slots


class Part:

    def __init__(self, base, first, last, tail, prep, xprep, steps=(0, 1)):
        self.base, self.first, self.last = base, first, last
        self.tail, self.prep, self.xprep, self.steps = tail, prep, xprep, steps
        self.slots = {}
        self.index = {}
        for x in steps:
            s = slots_of(None, x, tail, prep if x == 1 else True, xprep)
            self.slots[x] = s
            for slot in s:
                for u in slot:
                    self.index[u, x] = len(self.index)
        self.per = len(self.index)
        n = last - first + 1
        assert n == 1 or self.per % 3 == 0
        self.end = base + n * self.per

    def number(self, i, u, x):
        return self.base + (i - self.first) * self.per + self.index[u, x]

    def start(self, i):
        return self.base + (i - self.first) * self.per

    def bank(self, u, x):
        return (self.base + self.index[u, x]) % 3


def parts_after(base):
    parts = []

    def add(first, last, **k):
        parts.append(Part(parts[-1].end if parts else base, first, last, **k))

    add(-1, -1, tail=False, prep=True, xprep=False, steps=(1,))
    add(0, 0, tail=False, prep=True, xprep=True)
    add(1, ITERS - PAIRS - 1, tail=True, prep=True, xprep=True)
    for i in range(ITERS - PAIRS, ITERS - 1):
        add(i, i, tail=True, prep=True, xprep=False)
    add(ITERS - 1, ITERS - 1, tail=True, prep=False, xprep=False)
    return parts


def attention_block(nc, x_in, gn_scale, gn_bias, w_qkv, b_qkv, w_proj, b_proj,
                    ident_in, group_in, mask_in, out, w_dram):
    ctx = ExitStack()

    def sb(name, shape, dt=F32):
        return ctx.enter_context(nc.sbuf_tensor(name, shape, dt))

    def sem(name):
        return ctx.enter_context(nc.semaphore(name))

    with ctx:
        ident = sb("ident", [P, P])
        group_mean = sb("group_mean", [P, P])
        own_tile = sb("own_tile", [NS, T])
        xs = sb("xs", [P, T])
        xn_h = sb("xn_h", [P, 2 * KT * T], F32R)
        xn_l = sb("xn_l", [P, 2 * KT * T], F32R)
        w_qk = [sb(f"w_qk{x}", [P, 2 * C], F32R) for x in range(2)]
        w_v = sb("w_v", [P, 2 * C], F32R)
        w_p = sb("w_p", [P, 2 * C], F32R)
        a_q = [sb(f"a_q{x}", [P, T], F32R) for x in range(2)]
        a_k = [sb(f"a_k{x}", [P, T], F32R) for x in range(2)]
        b_q = [sb(f"b_q{x}", [P, T], F32R) for x in range(2)]
        b_k = [sb(f"b_k{x}", [P, T], F32R) for x in range(2)]
        v_f = sb("v_f", [P, T])
        v_t = [sb(f"v_t{x}", [P, NS * VW], F16) for x in range(2)]
        p_f = sb("p_f", [P, 4 * T])
        p_h = sb("p_h", [P, 4 * T], F16)
        p_l = sb("p_l", [P, 4 * T], F16)
        row_max = sb("row_max", [P, 2 * NS])
        neg_max = sb("neg_max", [P, NS])
        o_low = sb("o_low", [P, 9 * DH])
        o_sum = sb("o_sum", [P, 9 * DH])
        r_sum = sb("r_sum", [P, 9])
        o_n = sb("o_n", [P, NS * P])
        at_h = sb("at_h", [P, T], F32R)
        at_l = sb("at_l", [P, T], F32R)
        acc = sb("acc", [P, KT * T])
        qk_bias = sb("qk_bias", [P, HEADS])
        p_bias = sb("p_bias", [P, PAIRS * KT])
        v_bias = sb("v_bias", [P, PAIRS])
        v_inv = sb("v_inv", [P, PAIRS])
        v_scl = sb("v_scl", [P, PAIRS])
        b_cols = sb("b_cols", [P, 16])
        dots = sb("dots", [P, 16])
        bn = sb("bn", [P, 12])
        mv = sb("mv", [P, 2])
        g_mean = sb("g_mean", [P, 1])
        dev = sb("dev", [P, 1])
        var_in = sb("var_in", [P, 1])
        var_eps = sb("var_eps", [P, 1])
        rstd = sb("rstd", [P, 1])
        minus_half = sb("minus_half", [P, 1])
        p_shift = sb("p_shift", [P, 1])
        one_row = sb("one_row", [P, T // 2])

        logits = ctx.enter_context(nc.psum_tensor("logits", [P, T], F32))
        o_ps = ctx.enter_context(nc.psum_tensor("o_ps", [P, 3 * HALF], F32))
        fill = [ctx.enter_context(nc.psum_tensor(f"fill{k}", [P, HALF], F32)) for k in range(3)]

        const_loaded = sem("const_loaded")
        w_loaded = [sem(f"w_loaded{k}") for k in range(2)]
        const_set = sem("const_set")
        w_scaled = sem("w_scaled")
        w_steps = sem("w_steps")
        wt_hi = sem("wt_hi")
        wt_raw = sem("wt_raw")
        w_stored = [sem(f"w_stored{k}") for k in range(2)]
        fill_ready = sem("fill_ready")
        fill_free = sem("fill_free")
        wqk_in = [sem(f"wqk_in{x}") for x in range(2)]
        wv_in = sem("wv_in")
        wp_in = sem("wp_in")
        xs_in = sem("xs_in")
        acc_in = sem("acc_in")
        acc_out = sem("acc_out")
        dup_k = [sem(f"dup_k{x}") for x in range(2)]
        dup_q = [sem(f"dup_q{x}") for x in range(2)]
        logits_ready = sem("logits_ready")
        pv_done = sem("pv_done")
        exp_done = sem("exp_done")
        ph_done = sem("ph_done")
        pl_dve = sem("pl_dve")
        pl_pool = sem("pl_pool")
        qk_hi = sem("qk_hi")
        vt_hi = sem("vt_hi")
        at_hi = sem("at_hi")
        o_low_done = sem("o_low_done")
        r_done = sem("r_done")
        o_sum_done = sem("o_sum_done")
        o_n_done = sem("o_n_done")
        neg_done = sem("neg_done")
        bn_done = sem("bn_done")
        x_steps = sem("x_steps")
        rstd_done = sem("rstd_done")
        y_done = sem("y_done")
        xn_hi = sem("xn_hi")
        xn_lo = sem("xn_lo")

        raw = [p_f[:, k * HALF:(k + 1) * HALF] for k in range(2)]
        gamma = p_f[:, 2 * HALF:3 * HALF]
        beta = p_f[:, 3 * HALF:4 * HALF]
        scaled = [p_f[:, (4 + k) * HALF:(5 + k) * HALF] for k in range(2)]
        waste = p_f[:, 6 * HALF:7 * HALF]
        wt_f = p_f[:, 7 * HALF:8 * HALF]
        st_h = [at_h[:, k * HALF:(k + 1) * HALF] for k in range(2)]
        st_l = [at_l[:, k * HALF:(k + 1) * HALF] for k in range(2)]

        NQK, NV, NP = HEADS, PAIRS, KT
        NW = NQK + NV + NP

        def w_rows(n):
            if n < NQK:
                r = n * 3 * DH
                return [(w_qkv[r:r + P, :], b_qkv[r:r + P], 0, P)]
            if n < NQK + NV:
                return [(w_qkv[r:r + DH, :], b_qkv[r:r + DH], x * DH, DH)
                        for x in range(2) for r in [(2 * (n - NQK) + x) * 3 * DH + 2 * DH]]
            r = (n - NQK - NV) * P
            return [(w_proj[r:r + P, :], b_proj[r:r + P], 0, P)]

        def w_loads(n):
            return len(w_rows(n))

        set_up = []
        for n in range(NW):
            set_up.append(("wt", n))
            if n >= NQK + NV:
                set_up.append(("pb", n - NQK - NV))
        first_x = len(set_up)
        for j in range(KT):
            set_up += [("mean", j), ("var", j)]
        number_of = {u: n for n, u in enumerate(set_up)}
        parts = parts_after(len(set_up))
        epilogue = parts[-1].end

        def for_parts(eng, body):
            for part in parts:
                if part.first == part.last:
                    body(part, part.first)
                else:
                    with eng.Fori(part.first, part.last + 1) as i:
                        body(part, i)

        def wait(eng, s, value):
            if isinstance(value, int) and value <= 0:
                return
            eng.wait_ge(s, value)

        def o_tile(tt, a, b):
            at = (tt // OT_BANK) * HALF + (tt % OT_BANK) * VW
            return o_ps[:, at + a:at + b]

        def o_tiles(a, b):
            return o_ps[:, :].rearrange("p (g w) -> p g w", g=3)[:, :, 0:OT_BANK * VW] \
                .rearrange("p g (t w) -> p g t w", t=OT_BANK)[:, :, :, a:b]

        def nine(t):
            return t[:, :].rearrange("p (g t d) -> p g t d", g=3, t=OT_BANK)

        def v_cols(x, a, b):
            return v_t[x][:, :].rearrange("p (s w) -> p s w", s=NS)[:, :, a:b]

        def xn_at(t, batch, j, a, n):
            return t[:, bass.ds((batch % 2) * (KT * T) + j * T + a, n)]

        def wait_low(eng, n, s):
            k, s4 = (n, s - 4) if s >= 4 else (n - 1, s + 4)
            on_dve = s4 in PL_ON_DVE
            same = [t for t in range(NS) if (t in PL_ON_DVE) == on_dve]
            count = k * len(same) + same.index(s4) + 1
            wait(eng, pl_dve if on_dve else pl_pool, count)

        def wait_low_of(eng, n, s):
            on_dve = s in PL_ON_DVE
            same = [t for t in range(NS) if (t in PL_ON_DVE) == on_dve]
            eng.wait_ge(pl_dve if on_dve else pl_pool, n * len(same) + same.index(s) + 1)

        def wait_apart(eng, s, value):
            if isinstance(value, int):
                return wait(eng, s, value)
            value = eng.to_reg(value)
            eng.wait_ge(const_set, 6 + CONST_DVE)
            eng.wait_ge(s, value)

        block = ctx.enter_context(nc.Block())

        @block.sync
        def _(eng):
            eng.dma_start(ident[:, :], ident_in).then_inc(const_loaded, 16)
            eng.dma_start(group_mean[:, :], group_in).then_inc(const_loaded, 16)
            eng.dma_start(own_tile[:, :], mask_in).then_inc(const_loaded, 16)
            eng.dma_start(gamma, gn_scale.rearrange("(a n) -> a n", a=1).to_broadcast([P, C])).then_inc(const_loaded, 16)
            eng.dma_start(beta, gn_bias.rearrange("(a n) -> a n", a=1).to_broadcast([P, C])).then_inc(const_loaded, 16)
            for n in range(NW):
                for _, bias, p0, k in w_rows(n):
                    eng.dma_start(b_cols[p0:p0 + k, n:n + 1], bias.rearrange("(p a) -> p a", a=1))\
                        .then_inc(const_loaded, 16)
            for n in range(NW):
                if n >= 2:
                    eng.wait_ge(fill_ready, number_of["wt", n - 2] + 1)
                for src, _, p0, k in w_rows(n):
                    eng.dma_start(raw[n % 2][p0:p0 + k, :], src).then_inc(w_loaded[n % 2], 16)
                if n == 3:
                    for o in range(KT):
                        eng.dma_start(acc[:, o * T:(o + 1) * T], x_in[0, o * P:(o + 1) * P, :])\
                            .then_inc(acc_in, 16)
                    eng.dma_start(xs[:, :], x_in[0, 0:P, :]).then_inc(xs_in, 16)
            for j in range(1, KT):
                eng.wait_ge(xn_lo, j)
                eng.dma_start(xs[:, :], x_in[0, j * P:(j + 1) * P, :]).then_inc(xs_in, 16)
            for k in range(2):
                eng.wait_ge(w_stored[k], 16 * NW)
            eng.dma_start(w_qk[0][:, :].bitcast(F32), w_dram[0, :, 0, :]).then_inc(wqk_in[0], 16)
            eng.dma_start(w_v[:, :].bitcast(F32), w_dram[0, :, 2, :]).then_inc(wv_in, 16)

            def loads(part, i, closes=False):
                if part.xprep:
                    wait(eng, xn_lo, KT + i)
                    eng.dma_start(xs[:, :], x_in[i // PAIRS + 1, bass.ds((i % PAIRS) * P, P), :])\
                        .then_inc(xs_in, 16)
                if part.tail:
                    wait(eng, at_hi, 2 * (i - 1) + 1)
                    eng.dma_start(w_p[:, :].bitcast(F32), w_dram[(i - 1) % PAIRS, :, 3, :]).then_inc(wp_in, 16)
                if i_max(part) < ITERS - 1:
                    wait(eng, qk_hi, 4 * (2 * i + 1) + 4)
                    eng.dma_start(w_qk[1][:, :].bitcast(F32), w_dram[(i + 1) % PAIRS, :, 1, :]).then_inc(wqk_in[1], 16)
                if i_max(part) < ITERS - 2:
                    wait(eng, qk_hi, 4 * (2 * i + 2) + 4)
                    eng.dma_start(w_qk[0][:, :].bitcast(F32), w_dram[(i + 2) % PAIRS, :, 0, :]).then_inc(wqk_in[0], 16)
                    wait(eng, vt_hi, 2 * (i + 1) + 1)
                    eng.dma_start(w_v[:, :].bitcast(F32), w_dram[(i + 2) % PAIRS, :, 2, :]).then_inc(wv_in, 16)
                if closes:
                    finish_batch(part, i)

            def i_max(part):
                return part.last

            def finish_batch(part, i):
                b = i // PAIRS
                for o in range(KT):
                    u = ("proj", 2 * o + 1)
                    eng.wait_ge(fill_free, part.number(i, u, 0 if o < 2 else 1) + 1)
                    eng.dma_start(out[b - 1, o * P:(o + 1) * P, :], acc[:, o * T:(o + 1) * T])\
                        .then_inc(acc_out, 16)
                for o in range(KT):
                    eng.wait_ge(acc_out, 16 * KT * b)
                    eng.dma_start(acc[:, o * T:(o + 1) * T], x_in[b, o * P:(o + 1) * P, :])\
                        .then_inc(acc_in, 16)

            main = parts[2]
            for part in parts:
                if part is main:
                    with eng.Fori(0, B - 2) as b:
                        with eng.Fori(0, PAIRS - 1) as r:
                            loads(main, b * PAIRS + r + 1)
                        loads(main, b * PAIRS + PAIRS, closes=True)
                    with eng.Fori(0, PAIRS - 1) as r:
                        loads(main, r + (main.last - PAIRS + 2))
                else:
                    loads(part, part.first, closes=part.first == ITERS - PAIRS)
            eng.wait_ge(at_hi, 2 * (ITERS - 1) + 1)
            eng.dma_start(w_p[:, :].bitcast(F32), w_dram[PAIRS - 1, :, 3, :]).then_inc(wp_in, 16)
            for o in range(KT):
                eng.wait_ge(fill_free, epilogue + 2 + 2 * o + 2)
                eng.dma_start(out[B - 1, o * P:(o + 1) * P, :], acc[:, o * T:(o + 1) * T])\
                    .then_inc(acc_out, 16)
            eng.wait_ge(acc_out, 16 * KT * B)

        @block.gpsimd
        def _(eng):
            eng.memset(minus_half[:, :], -0.5).then_inc(const_set, 1)
            eng.memset(p_shift[:, :], P_SHIFT).then_inc(const_set, 1)
            eng.memset(one_row[:, :], 1.0).then_inc(const_set, 1)
            for x in range(2):
                eng.memset(v_t[x][:, :], 1.0).then_inc(const_set, 1)
            eng.memset(p_bias[:, :], 0.0).then_inc(const_set, 1)

            def inverse_std(n, number):
                eng.wait_ge(fill_free, number + 1)
                wait(eng, y_done, n)
                eng.tensor_tensor(rstd[:, :], var_eps[:, :], minus_half[:, :], ALU.pow)\
                    .then_inc(rstd_done, 1)

            def norm_tile(n, batch, j):
                eng.wait_ge(xn_hi, n + 1)
                eng.tensor_tensor(xn_at(xn_l, batch, j, 0, T), xs[:, :],
                                  xn_at(xn_h, batch, j, 0, T).bitcast(F32), ALU.subtract)\
                    .then_inc(xn_lo, 1)

            eng.wait_ge(const_set, 6 + CONST_DVE)
            for j in range(KT):
                inverse_std(j, number_of["var", j])
                norm_tile(j, 0, j)

            def low_parts(i, x, s):
                g = (2 * i + x) * NS + s
                eng.wait_ge(ph_done, g + 1)
                wait(eng, pv_done, g - 3)
                r = (s % 4) * T
                eng.tensor_tensor(p_l[:, r:r + T], p_f[:, r:r + T], p_h[:, r:r + T], ALU.subtract)\
                    .then_inc(pl_pool, 1)

            def body(part, i):
                if part.first < 0:
                    return
                for x in range(2):
                    for s in range(NS):
                        if s not in PL_ON_DVE:
                            low_parts(i, x, s)
                        if x == 0 and s == 2 and part.xprep:
                            inverse_std(i + KT, part.number(i, ("var",), 0))
                        if x == 0 and s == 4 and part.xprep:
                            norm_tile(i + KT, i // PAIRS + 1, i % PAIRS)

            for_parts(eng, body)

        @block.scalar
        def _(eng):
            eng.wait_ge(const_set, 6 + CONST_DVE)
            for n in range(NW):
                u = number_of["wt", n]
                eng.wait_ge(fill_ready, u + 1)
                if n >= 2:
                    eng.wait_ge(w_stored[n % 2], 32 * (n // 2))
                ps = fill[u % 3]
                if n < NQK:
                    eng.activation(st_h[n % 2], ps[:, :], ACT.Copy, scale=QK_SCALE).then_inc(wt_hi, 1)
                elif n < NQK + NV:
                    eng.activation(st_h[n % 2], ps[:, :], ACT.Copy).then_inc(wt_hi, 1)
                else:
                    o = n - NQK - NV
                    if o == 0:
                        eng.wait_ge(w_steps, W_STEPS)
                    if o >= 1:
                        eng.wait_ge(fill_ready, number_of["pb", o - 1] + 1)
                    eng.activation(wt_f, ps[:, :], ACT.Copy).then_inc(wt_raw, 1)
                    for k in range(KT):
                        a = eng.activation(st_h[n % 2][:, k * P:(k + 1) * P], ps[:, k * P:(k + 1) * P],
                                           ACT.Copy, scale=v_inv[:, k:k + 1])
                    a.then_inc(wt_hi, 1)
                wait(eng, wt_hi, n + 1)
                wait(eng, fill_free, u + 1)
                for part, st in enumerate((st_h, st_l)):
                    if n < NQK:
                        dst = w_dram[n // 2, :, n % 2, part * C:(part + 1) * C]
                        src = st[n % 2].bitcast(F32)
                    elif n < NQK + NV:
                        dst = w_dram[n - NQK, :, 2, part * C:(part + 1) * C]
                        src = st[n % 2].bitcast(F32)
                    else:
                        c = part * C + (n - NQK - NV) * P
                        dst = w_dram[:, :, 3, c:c + P].rearrange("k p c -> p k c")
                        src = st[n % 2].bitcast(F32).rearrange("p (k c) -> p k c", k=KT)
                    eng.dma_start(dst, src).then_inc(w_stored[n % 2], 16)

            def norm_tile(n, batch, j):
                wait_apart(eng, y_done, n + 1)
                eng.activation(xn_at(xn_h, batch, j, 0, T), xs[:, :], ACT.Copy).then_inc(xn_hi, 1)

            for j in range(KT):
                norm_tile(j, 0, j)

            def body(part, i):
                att = part.first >= 0
                for x in part.steps:
                    y = 1 - x
                    n = 2 * i + x
                    for s in range(NS):
                        g = n * NS + s
                        r = (s % 4) * T
                        if att:
                            eng.wait_ge(logits_ready, g + 1)
                            wait(eng, exp_done, g - 3)
                            wait(eng, ph_done, g - 3)
                            wait_low(eng, n, s)
                            eng.activation(p_f[:, r:r + T], logits[:, :], ACT.Exp, bias=p_shift[:, :])\
                                .then_inc(exp_done, 1)
                            eng.wait_ge(exp_done, g + 1)
                            wait(eng, pv_done, g - 3)
                            eng.activation(p_h[:, r:r + T], p_f[:, r:r + T], ACT.Copy).then_inc(ph_done, 1)
                        if s == 1 and (att and not (x == 0 and part.first == 0)):
                            eng.wait_ge(pv_done, n * NS)
                            wait(eng, o_sum_done, n - 1)
                            eng.wait_ge(r_done, n)
                            eng.activation(nine(o_low), o_tiles(DH + 1, 2 * DH + 1), ACT.Copy)\
                                .then_inc(o_low_done, 1)
                        for u in part.slots[x][s]:
                            ps = fill[part.bank(u, x)]
                            if u[0] in ("qk", "vt", "ot"):
                                wait_apart(eng, fill_ready, part.number(i, u, x) + 1)
                            if u[0] == "qk":
                                h, c = u[1], u[2] * HALF
                                head = (n + 1) % HEADS
                                for dst, lo, hi in ((a_q[h], 0, DH), (a_k[h], DH, P)):
                                    eng.activation(dst[lo:hi, c:c + HALF], ps[lo:hi, :], ACT.Identity,
                                                   bias=qk_bias[lo:hi, bass.ds(head, 1)])\
                                        .then_inc(qk_hi, 1)
                            elif u[0] == "vt":
                                eng.activation(v_cols(u[1], 0, DH),
                                               ps[:, :].rearrange("p (s d) -> p s d", s=NS), ACT.Copy)\
                                    .then_inc(vt_hi, 1)
                            elif u[0] == "ot":
                                c = u[1] * HALF
                                eng.activation(at_h[:, c:c + HALF], ps[:, :], ACT.Copy).then_inc(at_hi, 1)
                        if s == 1 and part.slots[x][1] and ("qk", y, 1) in part.slots[x][1]:
                            eng.wait_ge(qk_hi, 4 * (n + 1) + 4)
                            eng.dma_start(a_k[y][0:DH, :].bitcast(F32), a_k[y][DH:P, :].bitcast(F32)).then_inc(dup_k[y], 16)
                            eng.dma_start(b_q[y][0:DH, :].bitcast(F32), a_q[y][0:DH, :].bitcast(F32)).then_inc(dup_q[y], 16)
                        if x == 0 and s == 4 and part.xprep:
                            norm_tile(i + KT, i // PAIRS + 1, i % PAIRS)

            for_parts(eng, body)
            last = 2 * ITERS
            eng.wait_ge(pv_done, last * NS)
            eng.wait_ge(o_sum_done, last - 1)
            eng.wait_ge(r_done, last)
            eng.activation(nine(o_low), o_tiles(DH + 1, 2 * DH + 1), ACT.Copy).then_inc(o_low_done, 1)
            for h in range(2):
                u = epilogue + h
                eng.wait_ge(fill_ready, u + 1)
                eng.activation(at_h[:, h * HALF:(h + 1) * HALF], fill[u % 3][:, :], ACT.Copy)\
                    .then_inc(at_hi, 1)

        @block.vector
        def _(eng):
            eng.memset(o_ps[:, :], 1.0).then_inc(const_set, 1)
            eng.wait_ge(const_set, 6 + 1)
            for x in range(2):
                for u in range(2):
                    eng.tensor_copy(b_k[x][DH:DH + NS, u * HALF:(u + 1) * HALF], one_row[DH:DH + NS, :])\
                        .then_inc(const_set, 1)

            eng.wait_ge(const_loaded, 16 * (5 + NW + NV))
            count = 0

            def step(a):
                nonlocal count
                count += 1
                a.then_inc(w_steps, 1)
                eng.wait_ge(w_steps, count)

            seen = [0, 0]
            for n in range(NW):
                w = raw[n % 2]
                seen[n % 2] += 16 * w_loads(n)
                eng.wait_ge(w_loaded[n % 2], seen[n % 2])
                if n < NQK + NV:
                    if n >= 2:
                        eng.wait_ge(fill_ready, number_of["wt", n - 2] + 1)
                    step(eng.tensor_tensor_reduce(out=waste, in0=w, in1=beta, scale=1.0, scalar=0.0,
                                                  op0=ALU.mult, op1=ALU.add, accum_out=dots[:, n:n + 1]))
                    m = eng.tensor_tensor(scaled[n % 2], w, gamma, ALU.mult)
                    if n < NQK:
                        m.then_inc(w_scaled, 1)
                        step(eng.tensor_scalar(qk_bias[:, n:n + 1], dots[:, n:n + 1], b_cols[:, n:n + 1],
                                               QK_SCALE, ALU.add, ALU.mult))
                    else:
                        p = n - NQK
                        step(m)
                        step(eng.tensor_reduce(v_inv[:, p:p + 1], scaled[n % 2], AX.X, ALU.add,
                                               apply_absolute_value=True))
                        step(eng.tensor_scalar(v_inv[:, p:p + 1], v_inv[:, p:p + 1],
                                               XN_MAX / V_RANGE, 1e-30, ALU.mult, ALU.max))
                        step(eng.reciprocal(v_scl[:, p:p + 1], v_inv[:, p:p + 1]))
                        step(eng.tensor_scalar(v_bias[:, p:p + 1], dots[:, n:n + 1], b_cols[:, n:n + 1],
                                               None, ALU.add))
                        eng.tensor_scalar(scaled[n % 2], scaled[n % 2], v_scl[:, p:p + 1],
                                          None, ALU.mult).then_inc(w_scaled, 1)
                u = number_of["wt", n]
                ps = fill[u % 3]
                eng.wait_ge(wt_hi, n + 1)
                if n >= 2:
                    eng.wait_ge(w_stored[n % 2], 32 * (n // 2))
                if n < NQK:
                    eng.scalar_tensor_tensor(st_l[n % 2], ps[:, :], QK_SCALE, st_h[n % 2].bitcast(F32),
                                             ALU.mult, ALU.subtract).then_inc(fill_free, 1)
                elif n < NQK + NV:
                    eng.tensor_tensor(st_l[n % 2], ps[:, :], st_h[n % 2].bitcast(F32), ALU.subtract)\
                        .then_inc(fill_free, 1)
                else:
                    for k in range(KT):
                        a = eng.scalar_tensor_tensor(st_l[n % 2][:, k * P:(k + 1) * P],
                                                     ps[:, k * P:(k + 1) * P], v_inv[:, k:k + 1],
                                                     st_h[n % 2][:, k * P:(k + 1) * P].bitcast(F32),
                                                     ALU.mult, ALU.subtract)
                    a.then_inc(fill_free, 1)
                    o = n - NQK - NV
                    u = number_of["pb", o]
                    eng.wait_ge(fill_ready, u + 1)
                    eng.tensor_scalar(p_bias[:, o:o + 1], fill[u % 3][:, 0:1], b_cols[:, n:n + 1],
                                      None, ALU.add).then_inc(fill_free, 1)

            def stats(n):
                eng.wait_ge(xs_in, 16 * (n + 1))
                for h in range(2):
                    a = eng.bn_stats(bn[:, 6 * h:6 * h + 6], xs[:, h * HALF:(h + 1) * HALF])
                a.then_inc(bn_done, 1)
                wait_apart(eng, bn_done, 2 * n + 1)
                eng.bn_aggr(mv[:, :], bn[:, :]).then_inc(bn_done, 1)

            def mean_unit(n, number, bank):
                eng.wait_ge(fill_ready, number + 1)
                eng.tensor_copy(g_mean[:, :], fill[bank][:, 0:1]).then_inc(fill_free, 1)
                eng.wait_ge(fill_free, number + 1)
                eng.tensor_tensor(dev[:, :], mv[:, 0:1], g_mean[:, :], ALU.subtract).then_inc(x_steps, 1)
                eng.wait_ge(x_steps, 3 * n + 1)
                eng.tensor_tensor(var_in[:, :], dev[:, :], dev[:, :], ALU.mult).then_inc(x_steps, 1)
                eng.wait_ge(x_steps, 3 * n + 2)
                eng.tensor_tensor(var_in[:, :], var_in[:, :], mv[:, 1:2], ALU.add).then_inc(x_steps, 1)

            def var_unit(n, number, bank):
                eng.wait_ge(fill_ready, number + 1)
                eng.tensor_scalar(var_eps[:, :], fill[bank][:, 0:1], EPS, None, ALU.add)\
                    .then_inc(fill_free, 1)

            def normalise(n):
                eng.wait_ge(rstd_done, n + 1)
                eng.tensor_scalar(xs[:, :], xs[:, :], g_mean[:, 0:1], rstd[:, 0:1],
                                  ALU.subtract, ALU.mult).then_inc(y_done, 1)

            for j in range(KT):
                stats(j)
                mean_unit(j, number_of["mean", j], number_of["mean", j] % 3)
                var_unit(j, number_of["var", j], number_of["var", j] % 3)
                normalise(j)

            def low_parts(n, s):
                g = n * NS + s
                eng.wait_ge(ph_done, g + 1)
                wait(eng, pv_done, g - 3)
                r = (s % 4) * T
                eng.tensor_tensor(p_l[:, r:r + T], p_f[:, r:r + T], p_h[:, r:r + T], ALU.subtract)\
                    .then_inc(pl_dve, 1)

            def output(n):
                eng.wait_ge(pv_done, (n + 1) * NS)
                wait(eng, o_n_done, n)
                eng.reciprocal(r_sum[:, :].rearrange("p (g t a) -> p g t a", g=3, a=1),
                               o_tiles(DH, DH + 1)).then_inc(r_done, 1)
                eng.wait_ge(o_low_done, n + 1)
                eng.tensor_tensor(nine(o_sum), o_tiles(0, DH), nine(o_low), ALU.add)\
                    .then_inc(o_sum_done, 1)

            def normed(n, x):
                eng.wait_ge(o_sum_done, n + 1)
                eng.wait_ge(r_done, n + 1)
                dst = o_n[:, :].rearrange("p (t c) -> p t c", t=NS)[:, :, x * DH:(x + 1) * DH]
                src = o_sum[:, 0:NS * DH].rearrange("p (t d) -> p t d", t=NS)
                rs = r_sum[:, 0:NS].rearrange("p (t a) -> p t a", a=1).to_broadcast([P, NS, DH])
                eng.tensor_tensor(dst, src, rs, ALU.mult).then_inc(o_n_done, 1)

            def attention_sum(u, number, bank, part, i, b):
                o, h = u[1] // 2, u[1] % 2
                eng.wait_ge(fill_ready, number + 1)
                if u[1] == 0:
                    eng.wait_ge(acc_in, 16 * KT * (b + 1))
                c = o * T + h * HALF
                p = (i - 1) % PAIRS
                eng.scalar_tensor_tensor(acc[:, c:c + HALF], fill[bank][:, :],
                                         p_bias[:, bass.ds(p * KT + o, 1)], acc[:, c:c + HALF],
                                         ALU.add, ALU.add).then_inc(fill_free, 1)

            def unit(part, i, x, u):
                n = 2 * i + x
                number, bank = part.number(i, u, x), part.bank(u, x)
                ps = fill[bank]
                if u[0] == "qk":
                    h, half = u[1], u[2]
                    c = half * HALF
                    head = (n + 1) % HEADS
                    eng.wait_ge(qk_hi, 4 * (n + 1) + 2 * half + 1)
                    eng.scalar_tensor_tensor(a_q[h][DH:P, c:c + HALF], ps[0:DH, :],
                                             qk_bias[0:DH, bass.ds(head, 1)],
                                             a_q[h][0:DH, c:c + HALF].bitcast(F32), ALU.add, ALU.subtract)
                    eng.wait_ge(qk_hi, 4 * (n + 1) + 2 * half + 2)
                    eng.scalar_tensor_tensor(b_k[h][0:DH, c:c + HALF], ps[DH:P, :],
                                             qk_bias[DH:P, bass.ds(head, 1)],
                                             a_k[h][DH:P, c:c + HALF].bitcast(F32), ALU.add, ALU.subtract)\
                        .then_inc(fill_free, 1)
                elif u[0] == "max":
                    _, h, tt, half = u
                    eng.wait_ge(fill_ready, number + 1)
                    if (tt, half) == (0, 0):
                        wait(eng, neg_done, n + 1)
                    eng.tensor_reduce(row_max[:, 2 * tt + half:2 * tt + half + 1], ps[:, :], AX.X, ALU.max)\
                        .then_inc(fill_free, 1)
                    if (tt, half) == (NS - 1, 1):
                        eng.wait_ge(fill_free, number + 1)
                        eng.tensor_reduce(neg_max[:, :], row_max[:, :].rearrange("p (t h) -> p t h", h=2),
                                          AX.X, ALU.max, negate=True).then_inc(neg_done, 1)
                elif u[0] == "m":
                    h = u[1]
                    eng.wait_ge(fill_ready, number + 1)
                    src = ps[0:NS, 0:P].rearrange("j (a c) -> j a c", a=1).to_broadcast([NS, NS, P])
                    eng.tensor_tensor(b_q[h][DH:DH + NS, :].rearrange("j (a c) -> j a c", a=NS), src,
                                      own_tile[:, :].rearrange("j (a c) -> j a c", a=NS), ALU.mult)\
                        .then_inc(fill_free, 1)
                elif u[0] == "v":
                    eng.wait_ge(fill_ready, number + 1)
                    eng.tensor_copy(v_f[:, u[1] * HALF:(u[1] + 1) * HALF], ps[:, :]).then_inc(fill_free, 1)
                elif u[0] == "vt":
                    h = u[1]
                    eng.wait_ge(vt_hi, n + 2 if x == 0 else n + 2)
                    eng.tensor_tensor(v_cols(h, DH + 1, 2 * DH + 1),
                                      ps[:, :].rearrange("p (s d) -> p s d", s=NS),
                                      v_cols(h, 0, DH), ALU.subtract).then_inc(fill_free, 1)
                elif u[0] == "ot":
                    c = u[1] * HALF
                    eng.wait_ge(at_hi, 2 * (i - 1) + u[1] + 1)
                    eng.tensor_tensor(at_l[:, c:c + HALF], ps[:, :], at_h[:, c:c + HALF].bitcast(F32),
                                      ALU.subtract).then_inc(fill_free, 1)
                elif u[0] == "proj":
                    attention_sum(u, number, bank, part, i, (i - 1) // PAIRS)
                elif u[0] == "mean":
                    mean_unit(i + KT, number, bank)
                elif u[0] == "var":
                    var_unit(i + KT, number, bank)

            def body(part, i):
                att = part.first >= 0
                for x in part.steps:
                    n = 2 * i + x
                    for s in range(NS):
                        prev = NS - 1 if s == 0 else s - 1
                        first_step = part.first == 0 and x == 0
                        if att and prev in PL_ON_DVE and not (s == 0 and first_step):
                            low_parts(n - 1 if s == 0 else n, prev)
                        if x == 0 and s == 0 and part.xprep:
                            stats(i + KT)
                        if s == 1 and att and not first_step:
                            output(n - 1)
                            normed(n - 1, 1 - x)
                        for u in part.slots[x][s]:
                            unit(part, i, x, u)
                        if x == 0 and s == 3 and part.xprep:
                            normalise(i + KT)

            for_parts(eng, body)
            last = 2 * ITERS
            if NS - 1 in PL_ON_DVE:
                low_parts(last - 1, NS - 1)
            output(last - 1)
            normed(last - 1, 1)
            for h in range(2):
                u = epilogue + h
                c = h * HALF
                eng.wait_ge(at_hi, 2 * (ITERS - 1) + h + 1)
                eng.tensor_tensor(at_l[:, c:c + HALF], fill[u % 3][:, :], at_h[:, c:c + HALF].bitcast(F32),
                                  ALU.subtract).then_inc(fill_free, 1)
            for k in range(2 * KT):
                u = epilogue + 2 + k
                attention_sum(("proj", k), u, u % 3, None, ITERS, B - 1)

        @block.tensor
        def _(eng):
            def bank_free(number):
                wait(eng, fill_free, number - 2)

            eng.wait_ge(const_loaded, 16 * (5 + NW + NV))
            eng.wait_ge(const_set, 6 + CONST_DVE)
            for n in range(NW):
                u = number_of["wt", n]
                bank_free(u)
                if n < NQK + NV:
                    eng.wait_ge(w_scaled, n + 1)
                    src = scaled[n % 2]
                else:
                    eng.wait_ge(w_loaded[n % 2], W_SEEN[n])
                    src = raw[n % 2]
                for k in range(KT):
                    a = eng.transpose(fill[u % 3][:, k * P:(k + 1) * P], src[:, k * P:(k + 1) * P],
                                      ident[:, :])
                a.then_inc(fill_ready, 1)
                if n >= NQK + NV:
                    o = n - NQK - NV
                    u = number_of["pb", o]
                    bank_free(u)
                    eng.wait_ge(wt_raw, o + 1)
                    eng.wait_ge(w_steps, W_STEPS)
                    for k in range(KT):
                        a = eng.matmul(fill[u % 3][:, 0:1], wt_f[:, k * P:(k + 1) * P],
                                       v_bias[:, k:k + 1], start=k == 0, stop=k == KT - 1)
                    a.then_inc(fill_ready, 1)

            def mean_unit(n, number, bank):
                bank_free(number)
                eng.wait_ge(bn_done, 2 * n + 2)
                eng.matmul(fill[bank][:, 0:1], group_mean[:, :], mv[:, 0:1], start=True, stop=True)\
                    .then_inc(fill_ready, 1)

            def var_unit(n, number, bank):
                bank_free(number)
                eng.wait_ge(x_steps, 3 * n + 3)
                eng.matmul(fill[bank][:, 0:1], group_mean[:, :], var_in[:, :], start=True, stop=True)\
                    .then_inc(fill_ready, 1)

            for j in range(KT):
                mean_unit(j, number_of["mean", j], number_of["mean", j] % 3)
                var_unit(j, number_of["var", j], number_of["var", j] % 3)

            def project(ps, w, batch, half):
                products = [(k, wp, xp) for k in range(KT) for wp, xp in ((0, xn_h), (0, xn_l), (1, xn_h))]
                for m, (k, wp, xp) in enumerate(products):
                    c = wp * C + k * P
                    a = eng.matmul(ps[:, :], w[:, c:c + P], xn_at(xp, batch, k, half * HALF, HALF),
                                   start=m == 0, stop=m == len(products) - 1)
                return a

            def out_product(u, bank):
                o, h = u[1] // 2, u[1] % 2
                c = h * HALF
                for m, (wp, ap) in enumerate(((0, at_h), (0, at_l), (1, at_h))):
                    a = eng.matmul(fill[bank][:, :], w_p[:, wp * C + o * P:wp * C + (o + 1) * P],
                                   ap[:, c:c + HALF], start=m == 0, stop=m == 2)
                a.then_inc(fill_ready, 1)

            def turn_output(u, bank):
                for k in range(4):
                    tt = 4 * u[1] + k
                    a = eng.transpose(fill[bank][:, k * P:(k + 1) * P], o_n[:, tt * P:(tt + 1) * P],
                                      ident[:, :])
                a.then_inc(fill_ready, 1)

            def unit(part, i, x, u):
                number, bank = part.number(i, u, x), part.bank(u, x)
                n = 2 * i + x
                ps = fill[bank]
                if u[0] == "mean":
                    return mean_unit(i + KT, number, bank)
                if u[0] == "var":
                    return var_unit(i + KT, number, bank)
                after = {("vt", 0): ("v", 1), ("max", u[1], 0, 0): ("qk", u[1], 1),
                         ("proj", 0): ("ot", 1)}.get(u)
                due = part.index[u, x] - 2
                if after is not None:
                    due = max(due, part.index[after, x] + 1)
                (wait_apart if u[0] == "vt" else wait)(eng, fill_free, part.start(i) + due)
                if u[0] == "qk":
                    y, half = u[1], u[2]
                    pair = i + x
                    if half == 0:
                        eng.wait_ge(wqk_in[y], 16 * (pair + 1))
                        if y == 0:
                            eng.wait_ge(xn_lo, KT * (pair // PAIRS) + KT)
                    project(ps, w_qk[y], pair // PAIRS, half).then_inc(fill_ready, 1)
                elif u[0] == "v":
                    pair = i + 1
                    if u[1] == 0:
                        eng.wait_ge(wv_in, 16 * (pair + 1))
                    project(ps, w_v, pair // PAIRS, u[1]).then_inc(fill_ready, 1)
                elif u[0] == "vt":
                    h = u[1]
                    r = h * DH
                    for s in range(NS):
                        a = eng.transpose(ps[:, s * DH:(s + 1) * DH], v_f[r:r + DH, s * P:(s + 1) * P],
                                          ident[r:r + DH, r:r + DH])
                    a.then_inc(fill_ready, 1)
                elif u[0] == "max":
                    _, y, tt, half = u
                    if (tt, half) == (0, 0):
                        eng.wait_ge(dup_k[y], 16 * (i + x + 1))
                    eng.matmul(ps[:, :], a_q[y][:, tt * P:(tt + 1) * P],
                               a_k[y][:, half * HALF:(half + 1) * HALF], start=True, stop=True)\
                        .then_inc(fill_ready, 1)
                elif u[0] == "m":
                    eng.wait_ge(neg_done, n + 2)
                    eng.transpose(ps[0:NS, 0:P], neg_max[:, :], ident[:, :]).then_inc(fill_ready, 1)
                elif u[0] == "ot":
                    if u[1] == 0:
                        eng.wait_ge(o_n_done, 2 * i)
                    turn_output(u, bank)
                elif u[0] == "proj":
                    if u[1] == 0:
                        eng.wait_ge(wp_in, 16 * i)
                    out_product(u, bank)

            def scores(part, i, x, s):
                n = 2 * i + x
                g = n * NS + s
                if s == 0:
                    if x == 1:
                        eng.wait_ge(fill_free, part.number(i, ("m", 1), 0) + 1)
                    else:
                        eng.wait_ge(fill_free, part.start(i))
                    eng.wait_ge(dup_q[x], 16 * (i + 1))
                wait(eng, exp_done, g)
                for h in range(2):
                    c = h * HALF
                    eng.matmul(logits[:, c:c + HALF], a_k[x][:, s * P:(s + 1) * P], a_q[x][:, c:c + HALF],
                               start=True, stop=False)
                    a = eng.matmul(logits[:, c:c + HALF], b_k[x][0:DH + NS, s * P:(s + 1) * P],
                                   b_q[x][0:DH + NS, c:c + HALF], start=False, stop=True)
                a.then_inc(logits_ready, 1)

            def values(n, x, s):
                g = n * NS + s
                if s == 0:
                    wait(eng, o_sum_done, n)
                wait_low_of(eng, n, s)
                r = (s % 4) * T
                v = v_t[x]
                for tt in range(NS):
                    c = r + tt * P
                    eng.matmul(o_tile(tt, 0, 2 * DH + 1), p_h[:, c:c + P], v[:, s * VW:s * VW + 2 * DH + 1],
                               start=s == 0 and tt % OT_BANK == 0, stop=False, skip_group_check=True)
                    a = eng.matmul(o_tile(tt, 0, DH + 1), p_l[:, c:c + P], v[:, s * VW:s * VW + DH + 1],
                                   start=False, stop=s == NS - 1, skip_group_check=True)
                a.then_inc(pv_done, 1)

            def body(part, i):
                att = part.first >= 0
                for x in part.steps:
                    n = 2 * i + x
                    for s in range(NS):
                        if att:
                            scores(part, i, x, s)
                            if s < 2 and not (part.first == 0 and x == 0):
                                values(n - 1, 1 - x, NS - 2 + s)
                        for u in part.slots[x][s]:
                            unit(part, i, x, u)
                        if att and s >= 2:
                            values(n, x, s - 2)

            for_parts(eng, body)
            last = 2 * ITERS
            values(last - 1, 1, NS - 2)
            values(last - 1, 1, NS - 1)
            eng.wait_ge(o_n_done, last)
            for h in range(2):
                bank_free(epilogue + h)
                turn_output(("ot", h), (epilogue + h) % 3)
            eng.wait_ge(wp_in, 16 * ITERS)
            eng.wait_ge(fill_free, epilogue + 2)
            for k in range(2 * KT):
                u = epilogue + 2 + k
                bank_free(u)
                out_product(("proj", k), u % 3)


CONST_DVE = 1 + 4
_LOADS = [1] * HEADS + [2] * PAIRS + [1] * KT
W_SEEN = [16 * sum(_LOADS[m] for m in range(n % 2, n + 1, 2)) for n in range(len(_LOADS))]
W_STEPS = 2 * HEADS + 6 * PAIRS - 0


def kernel(x, L0_conv_gn_scale, L0_conv_gn_bias, L0_conv_w_qkv, L0_conv_b_qkv, L0_conv_w_proj,
           L0_conv_b_proj):
    import numpy as np
    from concourse import bacc
    from concourse.bass_utils import run_bass_kernel_spmd

    nc = bacc.Bacc("TRN2", target_bir_lowering=False, num_devices=1)
    ch = np.arange(P)
    per_group = C // GROUPS
    group = (ch[:, None] // per_group == ch[None, :] // per_group).astype(np.float32) / per_group
    mask = (np.arange(T)[None, :] // P == np.arange(NS)[:, None]).astype(np.float32)
    arrays = {
        "x": np.ascontiguousarray(x).reshape(B, C, T),
        "gn_scale": np.ascontiguousarray(L0_conv_gn_scale),
        "gn_bias": np.ascontiguousarray(L0_conv_gn_bias),
        "w_qkv": np.ascontiguousarray(L0_conv_w_qkv),
        "b_qkv": np.ascontiguousarray(L0_conv_b_qkv),
        "w_proj": np.ascontiguousarray(L0_conv_w_proj),
        "b_proj": np.ascontiguousarray(L0_conv_b_proj),
        "ident": np.eye(P, dtype=np.float32),
        "group_mean": group,
        "own_tile": mask,
    }
    arrays = {f"in_{k}": a for k, a in arrays.items()}
    args = [nc.dram_tensor(k, a.shape, F32, kind="ExternalInput").ap() for k, a in arrays.items()]
    out = nc.dram_tensor("out", (B, C, T), F32, kind="ExternalOutput").ap()
    w_dram = nc.dram_tensor("w_dram", (PAIRS, P, 4, 2 * C), F32, kind="Internal").ap()
    attention_block(nc, *args, out, w_dram)
    r = run_bass_kernel_spmd(nc, [arrays], core_ids=[0])
    return r.results[0]["out"].reshape(B, C, 32, 32)
```

```python
from contextlib import ExitStack

import concourse.bass as bass
from concourse import mybir

F32 = mybir.dt.float32
F32R = mybir.dt.float32r
F16 = mybir.dt.float16
ALU = mybir.AluOpType
ACT = mybir.ActivationFunctionType
AX = mybir.AxisListType

B, C, T = 16, 512, 1024
HEADS, DH = 8, 64
GROUPS, EPS = 32, 1e-5
P = 128
KT = C // P
PAIRS = HEADS // 2
ITERS = B * PAIRS
NS = T // P
HALF = 512
QK_SCALE = float(DH) ** -0.25
XN_MAX = 128.0
V_RANGE = 32768.0
P_SHIFT = 4 * 0.6931471805599453
VW = 2 * DH + 2
OT_BANK = 3

PL_ON_DVE = (7,)


MAX_EARLY = [(tt, 0) for tt in range(NS // 2)]
MAX_ORDER = MAX_EARLY + [(tt, u) for tt in range(NS) for u in (0, 1) if (tt, u) not in MAX_EARLY]


def slots_of(i_static, x, tail, prep, xprep):
    y = 1 - x
    row_maxima = iter([("max", y, tt, u) for tt, u in MAX_ORDER] if prep else [])

    def maxima(n):
        return [u for _, u in zip(range(n), row_maxima)]

    if x == 0:
        slots = [
            [("qk", y, 0)],
            [("vt", 1), ("qk", y, 1)] + [("mean",)] * xprep,
            maxima(4),
            maxima(3) + [("var",)] * xprep + [("ot", 0)] * tail,
            maxima(3) + [("ot", 1)] * tail,
            maxima(3) + [("proj", 0)] * tail,
            maxima(3) + [("proj", 1)] * tail,
            [("m", y)] + [("proj", 2), ("proj", 3)] * tail,
        ]
    else:
        slots = [
            [("qk", y, 0)] * prep + [("proj", 4)] * tail,
            [("qk", y, 1)] * prep + [("proj", 5)] * tail,
            [("proj", 6)] * tail + maxima(2),
            maxima(2) + [("v", 0)] * prep + maxima(1),
            maxima(2) + [("v", 1)] * prep + maxima(1),
            maxima(4) + [("vt", 0)] * prep,
            maxima(4) + [("proj", 7)] * tail,
            [("m", y)] * prep,
        ]
    return slots


class Part:

    def __init__(self, base, first, last, tail, prep, xprep, steps=(0, 1)):
        self.base, self.first, self.last = base, first, last
        self.tail, self.prep, self.xprep, self.steps = tail, prep, xprep, steps
        self.slots = {}
        self.index = {}
        for x in steps:
            s = slots_of(None, x, tail, prep if x == 1 else True, xprep)
            self.slots[x] = s
            for slot in s:
                for u in slot:
                    self.index[u, x] = len(self.index)
        self.per = len(self.index)
        n = last - first + 1
        assert n == 1 or self.per % 3 == 0
        self.end = base + n * self.per

    def number(self, i, u, x):
        return self.base + (i - self.first) * self.per + self.index[u, x]

    def start(self, i):
        return self.base + (i - self.first) * self.per

    def bank(self, u, x):
        return (self.base + self.index[u, x]) % 3


def parts_after(base):
    parts = []

    def add(first, last, **k):
        parts.append(Part(parts[-1].end if parts else base, first, last, **k))

    add(-1, -1, tail=False, prep=True, xprep=False, steps=(1,))
    add(0, 0, tail=False, prep=True, xprep=True)
    add(1, ITERS - PAIRS - 1, tail=True, prep=True, xprep=True)
    for i in range(ITERS - PAIRS, ITERS - 1):
        add(i, i, tail=True, prep=True, xprep=False)
    add(ITERS - 1, ITERS - 1, tail=True, prep=False, xprep=False)
    return parts


def attention_block(nc, x_in, gn_scale, gn_bias, w_qkv, b_qkv, w_proj, b_proj,
                    ident_in, group_in, mask_in, out, w_dram):
    ctx = ExitStack()

    def sb(name, shape, dt=F32):
        return ctx.enter_context(nc.sbuf_tensor(name, shape, dt))

    def sem(name):
        return ctx.enter_context(nc.semaphore(name))

    with ctx:
        ident = sb("ident", [P, P])
        group_mean = sb("group_mean", [P, P])
        own_tile = sb("own_tile", [NS, T])
        xs = sb("xs", [P, T])
        xn_h = sb("xn_h", [P, 2 * KT * T], F32R)
        xn_l = sb("xn_l", [P, 2 * KT * T], F32R)
        w_qk = [sb(f"w_qk{x}", [P, 2 * C], F32R) for x in range(2)]
        w_v = sb("w_v", [P, 2 * C], F32R)
        w_p = sb("w_p", [P, 2 * C], F32R)
        a_q = [sb(f"a_q{x}", [P, T], F32R) for x in range(2)]
        a_k = [sb(f"a_k{x}", [P, T], F32R) for x in range(2)]
        b_q = [sb(f"b_q{x}", [P, T], F32R) for x in range(2)]
        b_k = [sb(f"b_k{x}", [P, T], F32R) for x in range(2)]
        v_f = sb("v_f", [P, T])
        v_t = [sb(f"v_t{x}", [P, NS * VW], F16) for x in range(2)]
        p_f = sb("p_f", [P, 4 * T])
        p_h = sb("p_h", [P, 4 * T], F16)
        p_l = sb("p_l", [P, 4 * T], F16)
        row_max = sb("row_max", [P, 2 * NS])
        neg_max = sb("neg_max", [P, NS])
        o_low = sb("o_low", [P, 9 * DH])
        o_sum = sb("o_sum", [P, 9 * DH])
        r_sum = sb("r_sum", [P, 9])
        o_n = sb("o_n", [P, NS * P])
        at_h = sb("at_h", [P, T], F32R)
        at_l = sb("at_l", [P, T], F32R)
        acc = sb("acc", [P, KT * T])
        qk_bias = sb("qk_bias", [P, HEADS])
        p_bias = sb("p_bias", [P, PAIRS * KT])
        v_bias = sb("v_bias", [P, PAIRS])
        v_inv = sb("v_inv", [P, PAIRS])
        v_scl = sb("v_scl", [P, PAIRS])
        b_cols = sb("b_cols", [P, 16])
        dots = sb("dots", [P, 16])
        bn = sb("bn", [P, 12])
        mv = sb("mv", [P, 2])
        g_mean = sb("g_mean", [P, 1])
        dev = sb("dev", [P, 1])
        var_in = sb("var_in", [P, 1])
        var_eps = sb("var_eps", [P, 1])
        rstd = sb("rstd", [P, 1])
        minus_half = sb("minus_half", [P, 1])
        p_shift = sb("p_shift", [P, 1])
        one_row = sb("one_row", [P, T // 2])

        logits = ctx.enter_context(nc.psum_tensor("logits", [P, T], F32))
        o_ps = ctx.enter_context(nc.psum_tensor("o_ps", [P, 3 * HALF], F32))
        fill = [ctx.enter_context(nc.psum_tensor(f"fill{k}", [P, HALF], F32)) for k in range(3)]

        const_loaded = sem("const_loaded")
        w_loaded = [sem(f"w_loaded{k}") for k in range(2)]
        const_set = sem("const_set")
        w_scaled = sem("w_scaled")
        w_steps = sem("w_steps")
        wt_hi = sem("wt_hi")
        wt_raw = sem("wt_raw")
        w_stored = [sem(f"w_stored{k}") for k in range(2)]
        fill_ready = sem("fill_ready")
        fill_free = sem("fill_free")
        wqk_in = [sem(f"wqk_in{x}") for x in range(2)]
        wv_in = sem("wv_in")
        wp_in = sem("wp_in")
        xs_in = sem("xs_in")
        acc_in = sem("acc_in")
        acc_out = sem("acc_out")
        dup_q = [sem(f"dup_q{x}") for x in range(2)]
        logits_ready = sem("logits_ready")
        pv_done = sem("pv_done")
        exp_done = sem("exp_done")
        ph_done = sem("ph_done")
        pl_dve = sem("pl_dve")
        pl_pool = sem("pl_pool")
        qk_hi = sem("qk_hi")
        q_lo = sem("q_lo")
        vt_hi = sem("vt_hi")
        at_hi = sem("at_hi")
        o_low_done = sem("o_low_done")
        r_done = sem("r_done")
        o_sum_done = sem("o_sum_done")
        o_n_done = sem("o_n_done")
        neg_done = sem("neg_done")
        bn_done = sem("bn_done")
        x_steps = sem("x_steps")
        rstd_done = sem("rstd_done")
        y_done = sem("y_done")
        xn_hi = sem("xn_hi")
        xn_lo = sem("xn_lo")

        raw = [p_f[:, k * HALF:(k + 1) * HALF] for k in range(2)]
        gamma = p_f[:, 2 * HALF:3 * HALF]
        beta = p_f[:, 3 * HALF:4 * HALF]
        scaled = [p_f[:, (4 + k) * HALF:(5 + k) * HALF] for k in range(2)]
        waste = p_f[:, 6 * HALF:7 * HALF]
        wt_f = p_f[:, 7 * HALF:8 * HALF]
        st_h = [at_h[:, k * HALF:(k + 1) * HALF] for k in range(2)]
        st_l = [at_l[:, k * HALF:(k + 1) * HALF] for k in range(2)]

        NQK, NV, NP = HEADS, PAIRS, KT
        NW = NQK + NV + NP

        def w_rows(n):
            if n < NQK:
                r = n * 3 * DH
                return [(w_qkv[r:r + P, :], b_qkv[r:r + P], 0, P)]
            if n < NQK + NV:
                return [(w_qkv[r:r + DH, :], b_qkv[r:r + DH], x * DH, DH)
                        for x in range(2) for r in [(2 * (n - NQK) + x) * 3 * DH + 2 * DH]]
            r = (n - NQK - NV) * P
            return [(w_proj[r:r + P, :], b_proj[r:r + P], 0, P)]

        def w_loads(n):
            return len(w_rows(n))

        set_up = []
        for n in range(NW):
            set_up.append(("wt", n))
            if n >= NQK + NV:
                set_up.append(("pb", n - NQK - NV))
        first_x = len(set_up)
        for j in range(KT):
            set_up += [("mean", j), ("var", j)]
        number_of = {u: n for n, u in enumerate(set_up)}
        parts = parts_after(len(set_up))
        epilogue = parts[-1].end

        def for_parts(eng, body):
            for part in parts:
                if part.first == part.last:
                    body(part, part.first)
                else:
                    with eng.Fori(part.first, part.last + 1) as i:
                        body(part, i)

        def wait(eng, s, value):
            if isinstance(value, int) and value <= 0:
                return
            eng.wait_ge(s, value)

        def o_tile(tt, a, b):
            at = (tt // OT_BANK) * HALF + (tt % OT_BANK) * VW
            return o_ps[:, at + a:at + b]

        def o_tiles(a, b):
            return o_ps[:, :].rearrange("p (g w) -> p g w", g=3)[:, :, 0:OT_BANK * VW] \
                .rearrange("p g (t w) -> p g t w", t=OT_BANK)[:, :, :, a:b]

        def nine(t):
            return t[:, :].rearrange("p (g t d) -> p g t d", g=3, t=OT_BANK)

        def v_cols(x, a, b):
            return v_t[x][:, :].rearrange("p (s w) -> p s w", s=NS)[:, :, a:b]

        def xn_at(t, batch, j, a, n):
            return t[:, bass.ds((batch % 2) * (KT * T) + j * T + a, n)]

        def wait_low(eng, n, s):
            k, s4 = (n, s - 4) if s >= 4 else (n - 1, s + 4)
            on_dve = s4 in PL_ON_DVE
            same = [t for t in range(NS) if (t in PL_ON_DVE) == on_dve]
            count = k * len(same) + same.index(s4) + 1
            wait(eng, pl_dve if on_dve else pl_pool, count)

        def wait_low_of(eng, n, s):
            on_dve = s in PL_ON_DVE
            same = [t for t in range(NS) if (t in PL_ON_DVE) == on_dve]
            eng.wait_ge(pl_dve if on_dve else pl_pool, n * len(same) + same.index(s) + 1)

        def wait_apart(eng, s, value):
            if isinstance(value, int):
                return wait(eng, s, value)
            value = eng.to_reg(value)
            eng.wait_ge(const_set, 6 + CONST_DVE)
            eng.wait_ge(s, value)

        block = ctx.enter_context(nc.Block())

        @block.sync
        def _(eng):
            eng.dma_start(ident[:, :], ident_in).then_inc(const_loaded, 16)
            eng.dma_start(group_mean[:, :], group_in).then_inc(const_loaded, 16)
            eng.dma_start(own_tile[:, :], mask_in).then_inc(const_loaded, 16)
            eng.dma_start(gamma, gn_scale.rearrange("(a n) -> a n", a=1).to_broadcast([P, C])).then_inc(const_loaded, 16)
            eng.dma_start(beta, gn_bias.rearrange("(a n) -> a n", a=1).to_broadcast([P, C])).then_inc(const_loaded, 16)
            for n in range(NW):
                for _, bias, p0, k in w_rows(n):
                    eng.dma_start(b_cols[p0:p0 + k, n:n + 1], bias.rearrange("(p a) -> p a", a=1))\
                        .then_inc(const_loaded, 16)
            for n in range(NW):
                if n >= 2:
                    eng.wait_ge(fill_ready, number_of["wt", n - 2] + 1)
                for src, _, p0, k in w_rows(n):
                    eng.dma_start(raw[n % 2][p0:p0 + k, :], src).then_inc(w_loaded[n % 2], 16)
                if n == 3:
                    for o in range(KT):
                        eng.dma_start(acc[:, o * T:(o + 1) * T], x_in[0, o * P:(o + 1) * P, :])\
                            .then_inc(acc_in, 16)
                    eng.dma_start(xs[:, :], x_in[0, 0:P, :]).then_inc(xs_in, 16)
            for j in range(1, KT):
                eng.wait_ge(xn_lo, j)
                eng.dma_start(xs[:, :], x_in[0, j * P:(j + 1) * P, :]).then_inc(xs_in, 16)
            for k in range(2):
                eng.wait_ge(w_stored[k], 16 * NW)
            eng.dma_start(w_qk[0][:, :].bitcast(F32), w_dram[0, :, 0, :]).then_inc(wqk_in[0], 16)
            eng.dma_start(w_v[:, :].bitcast(F32), w_dram[0, :, 2, :]).then_inc(wv_in, 16)

            def loads(part, i, closes=False, more_x=True):
                if i_max(part) < ITERS - 1:
                    wait(eng, qk_hi, 6 * (2 * i + 1) + 6)
                    eng.dma_start(w_qk[1][:, :].bitcast(F32), w_dram[(i + 1) % PAIRS, :, 1, :]).then_inc(wqk_in[1], 16)
                if i_max(part) < ITERS - 2:
                    wait(eng, qk_hi, 6 * (2 * i + 2) + 6)
                    eng.dma_start(w_qk[0][:, :].bitcast(F32), w_dram[(i + 2) % PAIRS, :, 0, :]).then_inc(wqk_in[0], 16)
                    wait(eng, vt_hi, 2 * (i + 1) + 1)
                    eng.dma_start(w_v[:, :].bitcast(F32), w_dram[(i + 2) % PAIRS, :, 2, :]).then_inc(wv_in, 16)
                if part.first >= 0:
                    if part.tail:
                        wait(eng, fill_ready, part.number(i, ("proj", 2 * KT - 1), 1) + 1)
                    eng.dma_start(w_p[:, :].bitcast(F32), w_dram[i % PAIRS, :, 3, :]).then_inc(wp_in, 16)
                if more_x:
                    wait(eng, xn_lo, KT + i + 1)
                    k = i + 1
                    eng.dma_start(xs[:, :], x_in[k // PAIRS + 1, bass.ds((k % PAIRS) * P, P), :])\
                        .then_inc(xs_in, 16)
                if closes:
                    finish_batch(part, i)

            def i_max(part):
                return part.last

            def finish_batch(part, i):
                b = i // PAIRS
                for o in range(KT):
                    u = ("proj", 2 * o + 1)
                    eng.wait_ge(fill_free, part.number(i, u, 0 if o < 2 else 1) + 1)
                    eng.dma_start(out[b - 1, o * P:(o + 1) * P, :], acc[:, o * T:(o + 1) * T])\
                        .then_inc(acc_out, 16)
                for o in range(KT):
                    eng.wait_ge(acc_out, 16 * KT * b)
                    eng.dma_start(acc[:, o * T:(o + 1) * T], x_in[b, o * P:(o + 1) * P, :])\
                        .then_inc(acc_in, 16)

            main = parts[2]
            for part in parts:
                if part is main:
                    with eng.Fori(0, B - 2) as b:
                        with eng.Fori(0, PAIRS - 1) as r:
                            loads(main, b * PAIRS + r + 1)
                        loads(main, b * PAIRS + PAIRS, closes=True)
                    with eng.Fori(0, PAIRS - 2) as r:
                        loads(main, r + (main.last - PAIRS + 2))
                    loads(main, main.last, more_x=False)
                else:
                    loads(part, part.first, closes=part.first == ITERS - PAIRS,
                          more_x=part.first < main.first)
            for o in range(KT):
                eng.wait_ge(fill_free, epilogue + 2 + 2 * o + 2)
                eng.dma_start(out[B - 1, o * P:(o + 1) * P, :], acc[:, o * T:(o + 1) * T])\
                    .then_inc(acc_out, 16)
            eng.wait_ge(acc_out, 16 * KT * B)

        @block.gpsimd
        def _(eng):
            eng.memset(minus_half[:, :], -0.5).then_inc(const_set, 1)
            eng.memset(p_shift[:, :], P_SHIFT).then_inc(const_set, 1)
            eng.memset(one_row[:, :], 1.0).then_inc(const_set, 1)
            for x in range(2):
                eng.memset(v_t[x][:, :], 1.0).then_inc(const_set, 1)
            eng.memset(p_bias[:, :], 0.0).then_inc(const_set, 1)

            def inverse_std(n, number):
                eng.wait_ge(fill_free, number + 1)
                wait(eng, y_done, n)
                eng.tensor_tensor(rstd[:, :], var_eps[:, :], minus_half[:, :], ALU.pow)\
                    .then_inc(rstd_done, 1)

            def norm_tile(n, batch, j):
                eng.wait_ge(xn_hi, n + 1)
                eng.tensor_tensor(xn_at(xn_l, batch, j, 0, T), xs[:, :],
                                  xn_at(xn_h, batch, j, 0, T).bitcast(F32), ALU.subtract)\
                    .then_inc(xn_lo, 1)

            eng.wait_ge(const_set, 6 + CONST_DVE)
            for j in range(KT):
                inverse_std(j, number_of["var", j])
                norm_tile(j, 0, j)

            def low_parts(i, x, s):
                g = (2 * i + x) * NS + s
                eng.wait_ge(ph_done, g + 1)
                wait(eng, pv_done, g - 3)
                r = (s % 4) * T
                eng.tensor_tensor(p_l[:, r:r + T], p_f[:, r:r + T], p_h[:, r:r + T], ALU.subtract)\
                    .then_inc(pl_pool, 1)

            def body(part, i):
                if part.first < 0:
                    return
                for x in range(2):
                    for s in range(NS):
                        if s not in PL_ON_DVE:
                            low_parts(i, x, s)
                        if x == 0 and s == 3 and part.xprep:
                            inverse_std(i + KT, part.number(i, ("var",), 0))
                        if x == 0 and s == 5 and part.xprep:
                            norm_tile(i + KT, i // PAIRS + 1, i % PAIRS)

            for_parts(eng, body)

        @block.scalar
        def _(eng):
            eng.wait_ge(const_set, 6 + CONST_DVE)
            for n in range(NW):
                u = number_of["wt", n]
                eng.wait_ge(fill_ready, u + 1)
                if n >= 2:
                    eng.wait_ge(w_stored[n % 2], 32 * (n // 2))
                ps = fill[u % 3]
                if n < NQK:
                    eng.activation(st_h[n % 2], ps[:, :], ACT.Copy, scale=QK_SCALE).then_inc(wt_hi, 1)
                elif n < NQK + NV:
                    eng.activation(st_h[n % 2], ps[:, :], ACT.Copy).then_inc(wt_hi, 1)
                else:
                    o = n - NQK - NV
                    if o == 0:
                        eng.wait_ge(w_steps, W_STEPS)
                    if o >= 1:
                        eng.wait_ge(fill_ready, number_of["pb", o - 1] + 1)
                    eng.activation(wt_f, ps[:, :], ACT.Copy).then_inc(wt_raw, 1)
                    for k in range(KT):
                        a = eng.activation(st_h[n % 2][:, k * P:(k + 1) * P], ps[:, k * P:(k + 1) * P],
                                           ACT.Copy, scale=v_inv[:, k:k + 1])
                    a.then_inc(wt_hi, 1)
                wait(eng, wt_hi, n + 1)
                wait(eng, fill_free, u + 1)
                for part, st in enumerate((st_h, st_l)):
                    if n < NQK:
                        dst = w_dram[n // 2, :, n % 2, part * C:(part + 1) * C]
                        src = st[n % 2].bitcast(F32)
                    elif n < NQK + NV:
                        dst = w_dram[n - NQK, :, 2, part * C:(part + 1) * C]
                        src = st[n % 2].bitcast(F32)
                    else:
                        c = part * C + (n - NQK - NV) * P
                        dst = w_dram[:, :, 3, c:c + P].rearrange("k p c -> p k c")
                        src = st[n % 2].bitcast(F32).rearrange("p (k c) -> p k c", k=KT)
                    eng.dma_start(dst, src).then_inc(w_stored[n % 2], 16)

            def norm_tile(n, batch, j):
                wait_apart(eng, y_done, n + 1)
                eng.activation(xn_at(xn_h, batch, j, 0, T), xs[:, :], ACT.Copy).then_inc(xn_hi, 1)

            for j in range(KT):
                norm_tile(j, 0, j)

            def body(part, i):
                att = part.first >= 0
                for x in part.steps:
                    y = 1 - x
                    n = 2 * i + x
                    def high_parts(n, s):
                        g, r = n * NS + s, (s % 4) * T
                        eng.wait_ge(exp_done, g + 1)
                        wait(eng, pv_done, g - 3)
                        eng.activation(p_h[:, r:r + T], p_f[:, r:r + T], ACT.Copy).then_inc(ph_done, 1)

                    for s in range(NS):
                        g = n * NS + s
                        r = (s % 4) * T
                        if att:
                            eng.wait_ge(logits_ready, g + 1)
                            wait(eng, exp_done, g - 3)
                            wait(eng, ph_done, g - 3)
                            wait_low(eng, n, s)
                            eng.activation(p_f[:, r:r + T], logits[:, :], ACT.Exp, bias=p_shift[:, :])\
                                .then_inc(exp_done, 1)
                        if s == 1 and (att and not (x == 0 and part.first == 0)):
                            eng.wait_ge(pv_done, n * NS)
                            wait(eng, o_sum_done, n - 1)
                            eng.wait_ge(r_done, n)
                            eng.activation(nine(o_low), o_tiles(DH + 1, 2 * DH + 1), ACT.Copy)\
                                .then_inc(o_low_done, 1)
                        if att and s != 1:
                            high_parts(n, s)
                        for u in part.slots[x][s]:
                            ps = fill[part.bank(u, x)]
                            if u[0] in ("qk", "vt", "ot"):
                                wait_apart(eng, fill_ready, part.number(i, u, x) + 1)
                            if u[0] == "qk":
                                h, c = u[1], u[2] * HALF
                                head = (n + 1) % HEADS
                                for dst, to, lo in ((a_q[h], 0, 0), (a_k[h], DH, DH)):
                                    eng.activation(dst[to:to + DH, c:c + HALF], ps[lo:lo + DH, :],
                                                   ACT.Identity,
                                                   bias=qk_bias[lo:lo + DH, bass.ds(head, 1)])\
                                        .then_inc(qk_hi, 1)
                                eng.wait_ge(qk_hi, 6 * (n + 1) + 3 * u[2] + 2)
                                eng.activation(a_k[h][0:DH, c:c + HALF],
                                               a_k[h][DH:P, c:c + HALF].bitcast(F32), ACT.Copy)\
                                    .then_inc(qk_hi, 1)
                            elif u[0] == "vt":
                                eng.activation(v_cols(u[1], 0, DH),
                                               ps[:, :].rearrange("p (s d) -> p s d", s=NS), ACT.Copy)\
                                    .then_inc(vt_hi, 1)
                            elif u[0] == "ot":
                                c = u[1] * HALF
                                eng.activation(at_h[:, c:c + HALF], ps[:, :], ACT.Copy).then_inc(at_hi, 1)
                        if att and s == 1:
                            high_parts(n, s)
                        if s == 1 and part.slots[x][1] and ("qk", y, 1) in part.slots[x][1]:
                            eng.wait_ge(qk_hi, 6 * (n + 1) + 6)
                            eng.dma_start(b_q[y][0:DH, :].bitcast(F32), a_q[y][0:DH, :].bitcast(F32)).then_inc(dup_q[y], 16)
                        if x == 0 and s == 5 and part.xprep:
                            norm_tile(i + KT, i // PAIRS + 1, i % PAIRS)

            for_parts(eng, body)
            last = 2 * ITERS
            eng.wait_ge(pv_done, last * NS)
            eng.wait_ge(o_sum_done, last - 1)
            eng.wait_ge(r_done, last)
            eng.activation(nine(o_low), o_tiles(DH + 1, 2 * DH + 1), ACT.Copy).then_inc(o_low_done, 1)
            for h in range(2):
                u = epilogue + h
                eng.wait_ge(fill_ready, u + 1)
                eng.activation(at_h[:, h * HALF:(h + 1) * HALF], fill[u % 3][:, :], ACT.Copy)\
                    .then_inc(at_hi, 1)

        @block.vector
        def _(eng):
            eng.memset(o_ps[:, :], 1.0).then_inc(const_set, 1)
            eng.wait_ge(const_set, 6 + 1)
            for x in range(2):
                for u in range(2):
                    eng.tensor_copy(b_k[x][DH:DH + NS, u * HALF:(u + 1) * HALF], one_row[DH:DH + NS, :])\
                        .then_inc(const_set, 1)

            eng.wait_ge(const_loaded, 16 * (5 + NW + NV))
            count = 0

            def step(a):
                nonlocal count
                count += 1
                a.then_inc(w_steps, 1)
                eng.wait_ge(w_steps, count)

            seen = [0, 0]
            for n in range(NW):
                w = raw[n % 2]
                seen[n % 2] += 16 * w_loads(n)
                eng.wait_ge(w_loaded[n % 2], seen[n % 2])
                if n < NQK + NV:
                    if n >= 2:
                        eng.wait_ge(fill_ready, number_of["wt", n - 2] + 1)
                    step(eng.tensor_tensor_reduce(out=waste, in0=w, in1=beta, scale=1.0, scalar=0.0,
                                                  op0=ALU.mult, op1=ALU.add, accum_out=dots[:, n:n + 1]))
                    m = eng.tensor_tensor(scaled[n % 2], w, gamma, ALU.mult)
                    if n < NQK:
                        m.then_inc(w_scaled, 1)
                        step(eng.tensor_scalar(qk_bias[:, n:n + 1], dots[:, n:n + 1], b_cols[:, n:n + 1],
                                               QK_SCALE, ALU.add, ALU.mult))
                    else:
                        p = n - NQK
                        step(m)
                        step(eng.tensor_reduce(v_inv[:, p:p + 1], scaled[n % 2], AX.X, ALU.add,
                                               apply_absolute_value=True))
                        step(eng.tensor_scalar(v_inv[:, p:p + 1], v_inv[:, p:p + 1],
                                               XN_MAX / V_RANGE, 1e-30, ALU.mult, ALU.max))
                        step(eng.reciprocal(v_scl[:, p:p + 1], v_inv[:, p:p + 1]))
                        step(eng.tensor_scalar(v_bias[:, p:p + 1], dots[:, n:n + 1], b_cols[:, n:n + 1],
                                               None, ALU.add))
                        eng.tensor_scalar(scaled[n % 2], scaled[n % 2], v_scl[:, p:p + 1],
                                          None, ALU.mult).then_inc(w_scaled, 1)
                u = number_of["wt", n]
                ps = fill[u % 3]
                eng.wait_ge(wt_hi, n + 1)
                if n >= 2:
                    eng.wait_ge(w_stored[n % 2], 32 * (n // 2))
                if n < NQK:
                    eng.scalar_tensor_tensor(st_l[n % 2], ps[:, :], QK_SCALE, st_h[n % 2].bitcast(F32),
                                             ALU.mult, ALU.subtract).then_inc(fill_free, 1)
                elif n < NQK + NV:
                    eng.tensor_tensor(st_l[n % 2], ps[:, :], st_h[n % 2].bitcast(F32), ALU.subtract)\
                        .then_inc(fill_free, 1)
                else:
                    for k in range(KT):
                        a = eng.scalar_tensor_tensor(st_l[n % 2][:, k * P:(k + 1) * P],
                                                     ps[:, k * P:(k + 1) * P], v_inv[:, k:k + 1],
                                                     st_h[n % 2][:, k * P:(k + 1) * P].bitcast(F32),
                                                     ALU.mult, ALU.subtract)
                    a.then_inc(fill_free, 1)
                    o = n - NQK - NV
                    u = number_of["pb", o]
                    eng.wait_ge(fill_ready, u + 1)
                    eng.tensor_scalar(p_bias[:, o:o + 1], fill[u % 3][:, 0:1], b_cols[:, n:n + 1],
                                      None, ALU.add).then_inc(fill_free, 1)

            def stats(n):
                eng.wait_ge(xs_in, 16 * (n + 1))
                for h in range(2):
                    a = eng.bn_stats(bn[:, 6 * h:6 * h + 6], xs[:, h * HALF:(h + 1) * HALF])
                a.then_inc(bn_done, 1)
                wait_apart(eng, bn_done, 2 * n + 1)
                eng.bn_aggr(mv[:, :], bn[:, :]).then_inc(bn_done, 1)

            def mean_unit(n, number, bank):
                eng.wait_ge(fill_ready, number + 1)
                eng.tensor_copy(g_mean[:, :], fill[bank][:, 0:1]).then_inc(fill_free, 1)
                eng.wait_ge(fill_free, number + 1)
                eng.tensor_tensor(dev[:, :], mv[:, 0:1], g_mean[:, :], ALU.subtract).then_inc(x_steps, 1)
                eng.wait_ge(x_steps, 3 * n + 1)
                eng.tensor_tensor(var_in[:, :], dev[:, :], dev[:, :], ALU.mult).then_inc(x_steps, 1)
                eng.wait_ge(x_steps, 3 * n + 2)
                eng.tensor_tensor(var_in[:, :], var_in[:, :], mv[:, 1:2], ALU.add).then_inc(x_steps, 1)

            def var_unit(n, number, bank):
                eng.wait_ge(fill_ready, number + 1)
                eng.tensor_scalar(var_eps[:, :], fill[bank][:, 0:1], EPS, None, ALU.add)\
                    .then_inc(fill_free, 1)

            def normalise(n):
                eng.wait_ge(rstd_done, n + 1)
                eng.tensor_scalar(xs[:, :], xs[:, :], g_mean[:, 0:1], rstd[:, 0:1],
                                  ALU.subtract, ALU.mult).then_inc(y_done, 1)

            for j in range(KT):
                stats(j)
                mean_unit(j, number_of["mean", j], number_of["mean", j] % 3)
                var_unit(j, number_of["var", j], number_of["var", j] % 3)
                normalise(j)

            def low_parts(n, s):
                g = n * NS + s
                eng.wait_ge(ph_done, g + 1)
                wait(eng, pv_done, g - 3)
                r = (s % 4) * T
                eng.tensor_tensor(p_l[:, r:r + T], p_f[:, r:r + T], p_h[:, r:r + T], ALU.subtract)\
                    .then_inc(pl_dve, 1)

            def output(n):
                eng.wait_ge(pv_done, (n + 1) * NS)
                wait(eng, o_n_done, n)
                eng.reciprocal(r_sum[:, :].rearrange("p (g t a) -> p g t a", g=3, a=1),
                               o_tiles(DH, DH + 1)).then_inc(r_done, 1)
                eng.wait_ge(o_low_done, n + 1)
                eng.tensor_tensor(nine(o_sum), o_tiles(0, DH), nine(o_low), ALU.add)\
                    .then_inc(o_sum_done, 1)

            def normed(n, x):
                eng.wait_ge(o_sum_done, n + 1)
                eng.wait_ge(r_done, n + 1)
                dst = o_n[:, :].rearrange("p (t c) -> p t c", t=NS)[:, :, x * DH:(x + 1) * DH]
                src = o_sum[:, 0:NS * DH].rearrange("p (t d) -> p t d", t=NS)
                rs = r_sum[:, 0:NS].rearrange("p (t a) -> p t a", a=1).to_broadcast([P, NS, DH])
                eng.tensor_tensor(dst, src, rs, ALU.mult).then_inc(o_n_done, 1)

            def attention_sum(u, number, bank, part, i, b):
                o, h = u[1] // 2, u[1] % 2
                eng.wait_ge(fill_ready, number + 1)
                if u[1] == 0:
                    eng.wait_ge(acc_in, 16 * KT * (b + 1))
                c = o * T + h * HALF
                p = (i - 1) % PAIRS
                eng.scalar_tensor_tensor(acc[:, c:c + HALF], fill[bank][:, :],
                                         p_bias[:, bass.ds(p * KT + o, 1)], acc[:, c:c + HALF],
                                         ALU.add, ALU.add).then_inc(fill_free, 1)

            def unit(part, i, x, u):
                n = 2 * i + x
                number, bank = part.number(i, u, x), part.bank(u, x)
                ps = fill[bank]
                if u[0] == "qk":
                    h, half = u[1], u[2]
                    c = half * HALF
                    head = (n + 1) % HEADS
                    eng.wait_ge(qk_hi, 6 * (n + 1) + 3 * half + 1)
                    eng.scalar_tensor_tensor(a_q[h][DH:P, c:c + HALF], ps[0:DH, :],
                                             qk_bias[0:DH, bass.ds(head, 1)],
                                             a_q[h][0:DH, c:c + HALF].bitcast(F32), ALU.add, ALU.subtract)\
                        .then_inc(q_lo, 1)
                    eng.wait_ge(qk_hi, 6 * (n + 1) + 3 * half + 2)
                    eng.scalar_tensor_tensor(b_k[h][0:DH, c:c + HALF], ps[DH:P, :],
                                             qk_bias[DH:P, bass.ds(head, 1)],
                                             a_k[h][DH:P, c:c + HALF].bitcast(F32), ALU.add, ALU.subtract)\
                        .then_inc(fill_free, 1)
                elif u[0] == "max":
                    _, h, tt, half = u
                    eng.wait_ge(fill_ready, number + 1)
                    if (tt, half) == MAX_ORDER[0]:
                        wait(eng, neg_done, n + 1)
                    eng.tensor_reduce(row_max[:, 2 * tt + half:2 * tt + half + 1], ps[:, :], AX.X, ALU.max)\
                        .then_inc(fill_free, 1)
                    if (tt, half) == MAX_ORDER[-1]:
                        eng.wait_ge(fill_free, number + 1)
                        eng.tensor_reduce(neg_max[:, :], row_max[:, :].rearrange("p (t h) -> p t h", h=2),
                                          AX.X, ALU.max, negate=True).then_inc(neg_done, 1)
                elif u[0] == "m":
                    h = u[1]
                    eng.wait_ge(fill_ready, number + 1)
                    src = ps[0:NS, 0:P].rearrange("j (a c) -> j a c", a=1).to_broadcast([NS, NS, P])
                    eng.tensor_tensor(b_q[h][DH:DH + NS, :].rearrange("j (a c) -> j a c", a=NS), src,
                                      own_tile[:, :].rearrange("j (a c) -> j a c", a=NS), ALU.mult)\
                        .then_inc(fill_free, 1)
                elif u[0] == "v":
                    eng.wait_ge(fill_ready, number + 1)
                    eng.tensor_copy(v_f[:, u[1] * HALF:(u[1] + 1) * HALF], ps[:, :]).then_inc(fill_free, 1)
                elif u[0] == "vt":
                    h = u[1]
                    eng.wait_ge(vt_hi, n + 2 if x == 0 else n + 2)
                    eng.tensor_tensor(v_cols(h, DH + 1, 2 * DH + 1),
                                      ps[:, :].rearrange("p (s d) -> p s d", s=NS),
                                      v_cols(h, 0, DH), ALU.subtract).then_inc(fill_free, 1)
                elif u[0] == "ot":
                    c = u[1] * HALF
                    eng.wait_ge(at_hi, 2 * (i - 1) + u[1] + 1)
                    eng.tensor_tensor(at_l[:, c:c + HALF], ps[:, :], at_h[:, c:c + HALF].bitcast(F32),
                                      ALU.subtract).then_inc(fill_free, 1)
                elif u[0] == "proj":
                    attention_sum(u, number, bank, part, i, (i - 1) // PAIRS)
                elif u[0] == "mean":
                    mean_unit(i + KT, number, bank)
                elif u[0] == "var":
                    var_unit(i + KT, number, bank)

            def body(part, i):
                att = part.first >= 0
                for x in part.steps:
                    n = 2 * i + x
                    for s in range(NS):
                        prev = NS - 1 if s == 0 else s - 1
                        first_step = part.first == 0 and x == 0
                        if att and prev in PL_ON_DVE and not (s == 0 and first_step):
                            low_parts(n - 1 if s == 0 else n, prev)
                        if x == 0 and s == 0 and part.xprep:
                            stats(i + KT)
                        if s == 1 and att and not first_step:
                            output(n - 1)
                            normed(n - 1, 1 - x)
                        for u in part.slots[x][s]:
                            unit(part, i, x, u)
                        if x == 0 and s == 4 and part.xprep:
                            normalise(i + KT)

            for_parts(eng, body)
            last = 2 * ITERS
            if NS - 1 in PL_ON_DVE:
                low_parts(last - 1, NS - 1)
            output(last - 1)
            normed(last - 1, 1)
            for h in range(2):
                u = epilogue + h
                c = h * HALF
                eng.wait_ge(at_hi, 2 * (ITERS - 1) + h + 1)
                eng.tensor_tensor(at_l[:, c:c + HALF], fill[u % 3][:, :], at_h[:, c:c + HALF].bitcast(F32),
                                  ALU.subtract).then_inc(fill_free, 1)
            for k in range(2 * KT):
                u = epilogue + 2 + k
                attention_sum(("proj", k), u, u % 3, None, ITERS, B - 1)

        @block.tensor
        def _(eng):
            def bank_free(number):
                wait(eng, fill_free, number - 2)

            eng.wait_ge(const_loaded, 16 * (5 + NW + NV))
            eng.wait_ge(const_set, 6 + CONST_DVE)
            for n in range(NW):
                u = number_of["wt", n]
                bank_free(u)
                if n < NQK + NV:
                    eng.wait_ge(w_scaled, n + 1)
                    src = scaled[n % 2]
                else:
                    eng.wait_ge(w_loaded[n % 2], W_SEEN[n])
                    src = raw[n % 2]
                for k in range(KT):
                    a = eng.transpose(fill[u % 3][:, k * P:(k + 1) * P], src[:, k * P:(k + 1) * P],
                                      ident[:, :])
                a.then_inc(fill_ready, 1)
                if n >= NQK + NV:
                    o = n - NQK - NV
                    u = number_of["pb", o]
                    bank_free(u)
                    eng.wait_ge(wt_raw, o + 1)
                    eng.wait_ge(w_steps, W_STEPS)
                    for k in range(KT):
                        a = eng.matmul(fill[u % 3][:, 0:1], wt_f[:, k * P:(k + 1) * P],
                                       v_bias[:, k:k + 1], start=k == 0, stop=k == KT - 1)
                    a.then_inc(fill_ready, 1)

            def mean_unit(n, number, bank):
                bank_free(number)
                eng.wait_ge(bn_done, 2 * n + 2)
                eng.matmul(fill[bank][:, 0:1], group_mean[:, :], mv[:, 0:1], start=True, stop=True)\
                    .then_inc(fill_ready, 1)

            def var_unit(n, number, bank):
                bank_free(number)
                eng.wait_ge(x_steps, 3 * n + 3)
                eng.matmul(fill[bank][:, 0:1], group_mean[:, :], var_in[:, :], start=True, stop=True)\
                    .then_inc(fill_ready, 1)

            for j in range(KT):
                mean_unit(j, number_of["mean", j], number_of["mean", j] % 3)
                var_unit(j, number_of["var", j], number_of["var", j] % 3)

            def project(ps, w, batch, half, third):
                products = [(k, wp, xp) for k in range(KT) for wp, xp in ((0, xn_h), (0, xn_l), (1, xn_h))]
                n = len(products)
                for m in range(third * n // 3, (third + 1) * n // 3):
                    k, wp, xp = products[m]
                    c = wp * C + k * P
                    a = eng.matmul(ps[:, :], w[:, c:c + P], xn_at(xp, batch, k, half * HALF, HALF),
                                   start=m == 0, stop=m == n - 1)
                return a

            def out_product(u, bank):
                o, h = u[1] // 2, u[1] % 2
                c = h * HALF
                for m, (wp, ap) in enumerate(((0, at_h), (0, at_l), (1, at_h))):
                    a = eng.matmul(fill[bank][:, :], w_p[:, wp * C + o * P:wp * C + (o + 1) * P],
                                   ap[:, c:c + HALF], start=m == 0, stop=m == 2)
                a.then_inc(fill_ready, 1)

            def turn_output(u, bank):
                for k in range(4):
                    tt = 4 * u[1] + k
                    a = eng.transpose(fill[bank][:, k * P:(k + 1) * P], o_n[:, tt * P:(tt + 1) * P],
                                      ident[:, :])
                a.then_inc(fill_ready, 1)

            def unit(part, i, x, u):
                number, bank = part.number(i, u, x), part.bank(u, x)
                n = 2 * i + x
                ps = fill[bank]
                if u[0] == "mean":
                    return mean_unit(i + KT, number, bank)
                if u[0] == "var":
                    return var_unit(i + KT, number, bank)
                after = {("vt", 0): ("v", 1), ("proj", 0): ("ot", 1)}.get(u)
                due = part.index[u, x] - 2
                if after is not None:
                    due = max(due, part.index[after, x] + 1)
                (wait_apart if u[0] == "vt" else wait)(eng, fill_free, part.start(i) + due)
                if u[0] == "vt":
                    h = u[1]
                    r = h * DH
                    for s in range(NS):
                        a = eng.transpose(ps[:, s * DH:(s + 1) * DH], v_f[r:r + DH, s * P:(s + 1) * P],
                                          ident[r:r + DH, r:r + DH])
                    a.then_inc(fill_ready, 1)
                elif u[0] == "max":
                    _, y, tt, half = u
                    if (tt, half) == MAX_ORDER[0]:
                        eng.wait_ge(q_lo, 2 * (n + 1) + 1)
                        eng.wait_ge(qk_hi, 6 * (n + 1) + 3)
                    if (tt, half) == MAX_ORDER[len(MAX_EARLY)]:
                        eng.wait_ge(q_lo, 2 * (n + 1) + 2)
                        eng.wait_ge(qk_hi, 6 * (n + 1) + 6)
                    eng.matmul(ps[:, :], a_q[y][:, tt * P:(tt + 1) * P],
                               a_k[y][:, half * HALF:(half + 1) * HALF], start=True, stop=True)\
                        .then_inc(fill_ready, 1)
                elif u[0] == "m":
                    eng.wait_ge(neg_done, n + 2)
                    eng.transpose(ps[0:NS, 0:P], neg_max[:, :], ident[:, :]).then_inc(fill_ready, 1)
                elif u[0] == "ot":
                    if u[1] == 0:
                        eng.wait_ge(o_n_done, 2 * i)
                    turn_output(u, bank)
                elif u[0] == "proj":
                    if u[1] == 0:
                        eng.wait_ge(wp_in, 16 * i)
                    out_product(u, bank)

            def pieces_of(units):
                out = [(u, None) for u in units]
                for k, u in enumerate(units):
                    if u[0] in ("qk", "v"):
                        out[k] = (u, 2)
                        if k and units[k - 1][0] == "vt":
                            out[k:k] = [(u, 0), (u, 1)]
                            break
                        out.insert(max(0, k - 1), (u, 1))
                        out.insert(max(0, k - 2), (u, 0))
                        break
                return out

            def piece(part, i, x, u, third):
                if third is None:
                    unit(part, i, x, u)
                    return
                ps = fill[part.bank(u, x)]
                if u[0] == "qk":
                    w, pair, half, loaded = w_qk[u[1]], i + x, u[2], wqk_in[u[1]]
                else:
                    w, pair, half, loaded = w_v, i + 1, u[1], wv_in
                if third == 0:
                    wait(eng, fill_free, part.start(i) + part.index[u, x] - 2)
                    if half == 0:
                        eng.wait_ge(loaded, 16 * (pair + 1))
                        if u[:2] == ("qk", 0):
                            eng.wait_ge(xn_lo, KT * (pair // PAIRS) + KT)
                a = project(ps, w, pair // PAIRS, half, third)
                if third == 2:
                    a.then_inc(fill_ready, 1)

            def scores(part, i, x, s):
                n = 2 * i + x
                g = n * NS + s
                if s == 0:
                    if x == 1:
                        eng.wait_ge(fill_free, part.number(i, ("m", 1), 0) + 1)
                    else:
                        eng.wait_ge(fill_free, part.start(i))
                    eng.wait_ge(dup_q[x], 16 * (i + 1))
                wait(eng, exp_done, g)
                for h in range(2):
                    c = h * HALF
                    eng.matmul(logits[:, c:c + HALF], a_k[x][:, s * P:(s + 1) * P], a_q[x][:, c:c + HALF],
                               start=True, stop=False)
                    a = eng.matmul(logits[:, c:c + HALF], b_k[x][0:DH + NS, s * P:(s + 1) * P],
                                   b_q[x][0:DH + NS, c:c + HALF], start=False, stop=True)
                a.then_inc(logits_ready, 1)

            def values(n, x, s, first, end):
                g = n * NS + s
                if first == 0:
                    if s == 0:
                        wait(eng, o_sum_done, n)
                    wait_low_of(eng, n, s)
                r = (s % 4) * T
                v = v_t[x]
                for tt in range(first, end):
                    c = r + tt * P
                    eng.matmul(o_tile(tt, 0, DH + 1), p_l[:, c:c + P], v[:, s * VW:s * VW + DH + 1],
                               start=s == 0 and tt % OT_BANK == 0, stop=False, skip_group_check=True)
                    a = eng.matmul(o_tile(tt, 0, 2 * DH + 1), p_h[:, c:c + P], v[:, s * VW:s * VW + 2 * DH + 1],
                                   start=False, stop=s == NS - 1, skip_group_check=True)
                if end == NS:
                    a.then_inc(pv_done, 1)

            def body(part, i):
                att = part.first >= 0
                for x in part.steps:
                    n = 2 * i + x
                    for s in range(NS):
                        units = pieces_of(part.slots[x][s])
                        if not att:
                            for u in units:
                                piece(part, i, x, *u)
                            continue
                        pn, px, ps = (n, x, s - 2) if s >= 2 else (n - 1, 1 - x, NS - 2 + s)
                        has_values = not (part.first == 0 and x == 0 and s < 2)
                        done = 0 if has_values else NS
                        if s == 0 and has_values:
                            values(pn, px, ps, 0, NS)
                            done = NS
                        scores(part, i, x, s)
                        if s == 1 and has_values:
                            values(pn, px, ps, 0, NS)
                            done = NS
                        for k, u in enumerate(units):
                            piece(part, i, x, *u)
                            upto = (k + 1) * NS // len(units)
                            if upto > done:
                                values(pn, px, ps, done, upto)
                                done = upto
                        if done < NS:
                            values(pn, px, ps, done, NS)

            for_parts(eng, body)
            last = 2 * ITERS
            values(last - 1, 1, NS - 2, 0, NS)
            values(last - 1, 1, NS - 1, 0, NS)
            eng.wait_ge(o_n_done, last)
            for h in range(2):
                bank_free(epilogue + h)
                turn_output(("ot", h), (epilogue + h) % 3)
            eng.wait_ge(wp_in, 16 * ITERS)
            eng.wait_ge(fill_free, epilogue + 2)
            for k in range(2 * KT):
                u = epilogue + 2 + k
                bank_free(u)
                out_product(("proj", k), u % 3)


CONST_DVE = 1 + 4
_LOADS = [1] * HEADS + [2] * PAIRS + [1] * KT
W_SEEN = [16 * sum(_LOADS[m] for m in range(n % 2, n + 1, 2)) for n in range(len(_LOADS))]
W_STEPS = 2 * HEADS + 6 * PAIRS - 0


def kernel(x, L0_conv_gn_scale, L0_conv_gn_bias, L0_conv_w_qkv, L0_conv_b_qkv, L0_conv_w_proj,
           L0_conv_b_proj):
    import numpy as np
    from concourse import bacc
    from concourse.bass_utils import run_bass_kernel_spmd

    nc = bacc.Bacc("TRN2", target_bir_lowering=False, num_devices=1)
    ch = np.arange(P)
    per_group = C // GROUPS
    group = (ch[:, None] // per_group == ch[None, :] // per_group).astype(np.float32) / per_group
    mask = (np.arange(T)[None, :] // P == np.arange(NS)[:, None]).astype(np.float32)
    arrays = {
        "x": np.ascontiguousarray(x).reshape(B, C, T),
        "gn_scale": np.ascontiguousarray(L0_conv_gn_scale),
        "gn_bias": np.ascontiguousarray(L0_conv_gn_bias),
        "w_qkv": np.ascontiguousarray(L0_conv_w_qkv),
        "b_qkv": np.ascontiguousarray(L0_conv_b_qkv),
        "w_proj": np.ascontiguousarray(L0_conv_w_proj),
        "b_proj": np.ascontiguousarray(L0_conv_b_proj),
        "ident": np.eye(P, dtype=np.float32),
        "group_mean": group,
        "own_tile": mask,
    }
    arrays = {f"in_{k}": a for k, a in arrays.items()}
    args = [nc.dram_tensor(k, a.shape, F32, kind="ExternalInput").ap() for k, a in arrays.items()]
    out = nc.dram_tensor("out", (B, C, T), F32, kind="ExternalOutput").ap()
    w_dram = nc.dram_tensor("w_dram", (PAIRS, P, 4, 2 * C), F32, kind="Internal").ap()
    attention_block(nc, *args, out, w_dram)
    r = run_bass_kernel_spmd(nc, [arrays], core_ids=[0])
    return r.results[0]["out"].reshape(B, C, 32, 32)
```

```python
from contextlib import ExitStack

import concourse.bass as bass
from concourse import mybir

F32 = mybir.dt.float32
F32R = mybir.dt.float32r
F16 = mybir.dt.float16
ALU = mybir.AluOpType
ACT = mybir.ActivationFunctionType
AX = mybir.AxisListType

B, C, T = 16, 512, 1024
HEADS, DH = 8, 64
GROUPS, EPS = 32, 1e-5
P = 128
KT = C // P
PAIRS = HEADS // 2
ITERS = B * PAIRS
NS = T // P
HALF = 512
QK_SCALE = float(DH) ** -0.25
XN_MAX = 128.0
V_RANGE = 32768.0
P_SHIFT = 4 * 0.6931471805599453
VW = 2 * DH + 2
OT_BANK = 3

PL_ON_DVE = (5,)


MAX_EARLY = [(tt, 0) for tt in range(NS // 2)]
MAX_ORDER = MAX_EARLY + [(tt, u) for tt in range(NS) for u in (0, 1) if (tt, u) not in MAX_EARLY]


def slots_of(x, tail, prep, xprep):
    y = 1 - x
    row_maxima = iter([("max", y, tt, u) for tt, u in MAX_ORDER] if prep else [])

    def maxima(n):
        return [u for _, u in zip(range(n), row_maxima)]

    if x == 0:
        slots = [
            [("mean",)] * xprep + [("qk", y, 0)],
            [("qk", y, 1)] + [("var",)] * xprep + maxima(2),
            maxima(3),
            maxima(2) + [("ot", 0)] * tail + maxima(1),
            maxima(2) + [("ot", 1)] * tail + maxima(1),
            maxima(3) + [("proj", 0)] * tail,
            maxima(2) + [("proj", 1)] * tail,
            [("m", y)] + [("proj", 2)] * tail + [("vt", 1)] + [("proj", 3)] * tail,
        ]
    else:
        slots = [
            [("qk", y, 0)] * prep + [("proj", 4)] * tail,
            [("qk", y, 1)] * prep + [("proj", 5)] * tail,
            [("proj", 6)] * tail + maxima(2),
            maxima(2) + [("v", 0)] * prep + maxima(2),
            maxima(2) + [("v", 1)] * prep + maxima(2),
            maxima(2) + [("vt", 0)] * prep + maxima(1),
            maxima(3) + [("proj", 7)] * tail,
            [("m", y)] * prep,
        ]
    return slots


class Part:

    def __init__(self, base, first, last, tail, prep, xprep, steps=(0, 1)):
        self.base, self.first, self.last = base, first, last
        self.tail, self.prep, self.xprep, self.steps = tail, prep, xprep, steps
        self.slots = {}
        self.index = {}
        for x in steps:
            s = slots_of(x, tail, prep if x == 1 else True, xprep)
            self.slots[x] = s
            for slot in s:
                for u in slot:
                    self.index[u, x] = len(self.index)
        self.per = len(self.index)
        n = last - first + 1
        assert n == 1 or self.per % 3 == 0
        self.end = base + n * self.per

    def number(self, i, u, x):
        return self.base + (i - self.first) * self.per + self.index[u, x]

    def start(self, i):
        return self.base + (i - self.first) * self.per

    def bank(self, u, x):
        return (self.base + self.index[u, x]) % 3


def parts_after(base):
    parts = []

    def add(first, last, **k):
        parts.append(Part(parts[-1].end if parts else base, first, last, **k))

    add(-1, -1, tail=False, prep=True, xprep=False, steps=(1,))
    add(0, 0, tail=False, prep=True, xprep=True)
    add(1, ITERS - PAIRS - 1, tail=True, prep=True, xprep=True)
    for i in range(ITERS - PAIRS, ITERS - 1):
        add(i, i, tail=True, prep=True, xprep=False)
    add(ITERS - 1, ITERS - 1, tail=True, prep=False, xprep=False)
    return parts


def attention_block(nc, x_in, gn_scale, gn_bias, w_qkv, b_qkv, w_proj, b_proj,
                    ident_in, group_in, mask_in, out, w_dram):
    ctx = ExitStack()

    def sb(name, shape, dt=F32):
        return ctx.enter_context(nc.sbuf_tensor(name, shape, dt))

    def sem(name):
        return ctx.enter_context(nc.semaphore(name))

    with ctx:
        ident = sb("ident", [P, P])
        group_mean = sb("group_mean", [P, P])
        own_tile = sb("own_tile", [NS, T])
        xs = sb("xs", [P, T])
        xn_h = sb("xn_h", [P, 2 * KT * T], F32R)
        xn_l = sb("xn_l", [P, 2 * KT * T], F32R)
        w_qk = [sb(f"w_qk{x}", [P, 2 * C], F32R) for x in range(2)]
        w_v = sb("w_v", [P, 2 * C], F32R)
        w_p = sb("w_p", [P, 2 * C], F32R)
        a_q = [sb(f"a_q{x}", [P, T], F32R) for x in range(2)]
        a_k = [sb(f"a_k{x}", [P, T], F32R) for x in range(2)]
        b_q = [sb(f"b_q{x}", [P, T], F32R) for x in range(2)]
        b_k = [sb(f"b_k{x}", [P, T], F32R) for x in range(2)]
        v_f = sb("v_f", [P, T])
        v_t = [sb(f"v_t{x}", [P, NS * VW], F16) for x in range(2)]
        p_f = sb("p_f", [P, 4 * T])
        p_h = sb("p_h", [P, 4 * T], F16)
        p_l = sb("p_l", [P, 4 * T], F16)
        row_max = sb("row_max", [P, 2 * NS])
        neg_max = sb("neg_max", [P, NS])
        o_low = sb("o_low", [P, 9 * DH])
        o_sum = sb("o_sum", [P, 9 * DH])
        r_sum = sb("r_sum", [P, 9])
        o_n = sb("o_n", [P, NS * P])
        at_h = sb("at_h", [P, T], F32R)
        at_l = sb("at_l", [P, T], F32R)
        acc = sb("acc", [P, KT * T])
        qk_bias = sb("qk_bias", [P, HEADS])
        p_bias = sb("p_bias", [P, PAIRS * KT])
        v_bias = sb("v_bias", [P, PAIRS])
        v_inv = sb("v_inv", [P, PAIRS])
        v_scl = sb("v_scl", [P, PAIRS])
        b_cols = sb("b_cols", [P, 16])
        dots = sb("dots", [P, 16])
        bn = sb("bn", [P, 12])
        mv = sb("mv", [P, 2])
        g_mean = sb("g_mean", [P, 1])
        dev = sb("dev", [P, 1])
        var_in = sb("var_in", [P, 1])
        var_eps = sb("var_eps", [P, 1])
        rstd = sb("rstd", [P, 1])
        minus_half = sb("minus_half", [P, 1])
        p_shift = sb("p_shift", [P, 1])
        one_row = sb("one_row", [P, T // 2])

        logits = ctx.enter_context(nc.psum_tensor("logits", [P, T], F32))
        o_ps = ctx.enter_context(nc.psum_tensor("o_ps", [P, 3 * HALF], F32))
        fill = [ctx.enter_context(nc.psum_tensor(f"fill{k}", [P, HALF], F32)) for k in range(3)]

        const_loaded = sem("const_loaded")
        w_loaded = [sem(f"w_loaded{k}") for k in range(2)]
        const_set = sem("const_set")
        w_scaled = sem("w_scaled")
        w_steps = sem("w_steps")
        wt_hi = sem("wt_hi")
        wt_raw = sem("wt_raw")
        w_stored = [sem(f"w_stored{k}") for k in range(2)]
        fill_ready = sem("fill_ready")
        fill_free = sem("fill_free")
        wqk_in = [sem(f"wqk_in{x}") for x in range(2)]
        wv_in = sem("wv_in")
        wp_in = sem("wp_in")
        xs_in = sem("xs_in")
        acc_in = sem("acc_in")
        acc_out = sem("acc_out")
        dup_q = [sem(f"dup_q{x}") for x in range(2)]
        logits_ready = sem("logits_ready")
        pv_done = sem("pv_done")
        exp_done = sem("exp_done")
        ph_done = sem("ph_done")
        pl_dve = sem("pl_dve")
        pl_pool = sem("pl_pool")
        qk_hi = sem("qk_hi")
        k_copied = sem("k_copied")
        q_lo = sem("q_lo")
        vt_hi = sem("vt_hi")
        at_hi = sem("at_hi")
        o_low_done = sem("o_low_done")
        r_done = sem("r_done")
        o_sum_done = sem("o_sum_done")
        o_n_done = sem("o_n_done")
        neg_done = sem("neg_done")
        bn_done = sem("bn_done")
        x_steps = sem("x_steps")
        rstd_done = sem("rstd_done")
        y_done = sem("y_done")
        xn_hi = sem("xn_hi")
        xn_lo = sem("xn_lo")

        raw = [p_f[:, k * HALF:(k + 1) * HALF] for k in range(2)]
        gamma = p_f[:, 2 * HALF:3 * HALF]
        beta = p_f[:, 3 * HALF:4 * HALF]
        scaled = [p_f[:, (4 + k) * HALF:(5 + k) * HALF] for k in range(2)]
        waste = p_f[:, 6 * HALF:7 * HALF]
        wt_f = p_f[:, 7 * HALF:8 * HALF]
        st_h = [at_h[:, k * HALF:(k + 1) * HALF] for k in range(2)]
        st_l = [at_l[:, k * HALF:(k + 1) * HALF] for k in range(2)]

        NQK, NV, NP = HEADS, PAIRS, KT
        NW = NQK + NV + NP
        CONST_LOADS = 5 + 4

        def w_rows(n):
            if n < NQK:
                r = n * 3 * DH
                return [(w_qkv[r:r + P, :], 0, P)]
            if n < NQK + NV:
                return [(w_qkv[r:r + DH, :], x * DH, DH)
                        for x in range(2) for r in [(2 * (n - NQK) + x) * 3 * DH + 2 * DH]]
            r = (n - NQK - NV) * P
            return [(w_proj[r:r + P, :], 0, P)]

        set_up = []
        for n in range(NW):
            set_up.append(("wt", n))
            if n >= NQK + NV:
                set_up.append(("pb", n - NQK - NV))
        for j in range(KT):
            set_up += [("mean", j), ("var", j)]
        number_of = {u: n for n, u in enumerate(set_up)}
        parts = parts_after(len(set_up))
        epilogue = parts[-1].end

        def for_parts(eng, body):
            for part in parts:
                if part.first == part.last:
                    body(part, part.first)
                else:
                    with eng.Fori(part.first, part.last + 1) as i:
                        body(part, i)

        def wait(eng, s, value):
            if isinstance(value, int) and value <= 0:
                return
            eng.wait_ge(s, value)

        def o_tile(tt, a, b):
            at = (tt // OT_BANK) * HALF + (tt % OT_BANK) * VW
            return o_ps[:, at + a:at + b]

        def o_tiles(a, b):
            return o_ps[:, :].rearrange("p (g w) -> p g w", g=3)[:, :, 0:OT_BANK * VW] \
                .rearrange("p g (t w) -> p g t w", t=OT_BANK)[:, :, :, a:b]

        def nine(t):
            return t[:, :].rearrange("p (g t d) -> p g t d", g=3, t=OT_BANK)

        def v_cols(x, a, b):
            return v_t[x][:, :].rearrange("p (s w) -> p s w", s=NS)[:, :, a:b]

        def xn_at(t, batch, j, a, n):
            return t[:, bass.ds((batch % 2) * (KT * T) + j * T + a, n)]

        def first_y(j):
            return (xs, v_f)[j % 2]

        def wait_low(eng, n, s):
            k, s4 = (n, s - 4) if s >= 4 else (n - 1, s + 4)
            on_dve = s4 in PL_ON_DVE
            same = [t for t in range(NS) if (t in PL_ON_DVE) == on_dve]
            count = k * len(same) + same.index(s4) + 1
            wait(eng, pl_dve if on_dve else pl_pool, count)

        def wait_low_of(eng, n, s):
            on_dve = s in PL_ON_DVE
            same = [t for t in range(NS) if (t in PL_ON_DVE) == on_dve]
            eng.wait_ge(pl_dve if on_dve else pl_pool, n * len(same) + same.index(s) + 1)

        def wait_apart(eng, s, value):
            if isinstance(value, int):
                return wait(eng, s, value)
            value = eng.to_reg(value)
            eng.wait_ge(const_set, 6 + CONST_DVE)
            eng.wait_ge(s, value)

        block = ctx.enter_context(nc.Block())

        @block.sync
        def _(eng):
            eng.dma_start(ident[:, :], ident_in).then_inc(const_loaded, 16)
            eng.dma_start(group_mean[:, :], group_in).then_inc(const_loaded, 16)
            eng.dma_start(own_tile[:, :], mask_in).then_inc(const_loaded, 16)
            eng.dma_start(gamma, gn_scale.rearrange("(a n) -> a n", a=1).to_broadcast([P, C])).then_inc(const_loaded, 16)
            eng.dma_start(beta, gn_bias.rearrange("(a n) -> a n", a=1).to_broadcast([P, C])).then_inc(const_loaded, 16)
            of_head = b_qkv.rearrange("(n r a) -> r n a", n=HEADS, a=1)
            of_pair = b_qkv.rearrange("(n x r a) -> x r n a", n=PAIRS, x=2, a=1)
            to = b_cols[:, :].rearrange("p (n a) -> p n a", a=1)
            eng.dma_start(to[:, 0:NQK], of_head[0:P], allow_slow_non_contiguous=True).then_inc(const_loaded, 16)
            for x in range(2):
                eng.dma_start(to[x * DH:(x + 1) * DH, NQK:NQK + NV], of_pair[x, 2 * DH:3 * DH],
                              allow_slow_non_contiguous=True)\
                    .then_inc(const_loaded, 16)
            eng.dma_start(to[:, NQK + NV:NW], b_proj.rearrange("(n r a) -> r n a", n=NP, a=1),
                          allow_slow_non_contiguous=True)\
                .then_inc(const_loaded, 16)
            for n in range(NW):
                if n >= 2:
                    eng.wait_ge(fill_ready, number_of["wt", n - 2] + 1)
                for src, p0, k in w_rows(n):
                    eng.dma_start(raw[n % 2][p0:p0 + k, :], src).then_inc(w_loaded[n % 2], 16)
                if n == 3:
                    for o in range(KT):
                        eng.dma_start(acc[:, o * T:(o + 1) * T], x_in[0, o * P:(o + 1) * P, :])\
                            .then_inc(acc_in, 16)
            for k in range(2):
                eng.wait_ge(w_stored[k], 16 * NW)
            eng.dma_start(w_qk[0][:, :].bitcast(F32), w_dram[0, :, 0, :]).then_inc(wqk_in[0], 16)
            eng.dma_start(w_v[:, :].bitcast(F32), w_dram[0, :, 2, :]).then_inc(wv_in, 16)

            def loads(part, i, closes=False, more_x=True):
                if part.last < ITERS - 1:
                    wait(eng, qk_hi, 4 * (2 * i + 1) + 4)
                    eng.dma_start(w_qk[1][:, :].bitcast(F32), w_dram[(i + 1) % PAIRS, :, 1, :]).then_inc(wqk_in[1], 16)
                if more_x:
                    wait(eng, xn_lo, KT + i + 1)
                    k = i + 1
                    eng.dma_start(xs[:, :], x_in[k // PAIRS + 1, bass.ds((k % PAIRS) * P, P), :])\
                        .then_inc(xs_in, 16)
                if part.last < ITERS - 2:
                    wait(eng, qk_hi, 4 * (2 * i + 2) + 4)
                    eng.dma_start(w_qk[0][:, :].bitcast(F32), w_dram[(i + 2) % PAIRS, :, 0, :]).then_inc(wqk_in[0], 16)
                    wait(eng, vt_hi, 2 * (i + 1) + 1)
                    eng.dma_start(w_v[:, :].bitcast(F32), w_dram[(i + 2) % PAIRS, :, 2, :]).then_inc(wv_in, 16)
                if part.first >= 0:
                    if part.tail:
                        wait(eng, fill_ready, part.number(i, ("proj", 2 * KT - 1), 1) + 1)
                    eng.dma_start(w_p[:, :].bitcast(F32), w_dram[i % PAIRS, :, 3, :]).then_inc(wp_in, 16)
                if closes:
                    finish_batch(part, i)

            def finish_batch(part, i):
                b = i // PAIRS
                for o in range(KT):
                    u = ("proj", 2 * o + 1)
                    eng.wait_ge(fill_free, part.number(i, u, 0 if o < 2 else 1) + 1)
                    eng.dma_start(out[b - 1, o * P:(o + 1) * P, :], acc[:, o * T:(o + 1) * T])\
                        .then_inc(acc_out, 16)
                for o in range(KT):
                    eng.wait_ge(acc_out, 16 * KT * b)
                    eng.dma_start(acc[:, o * T:(o + 1) * T], x_in[b, o * P:(o + 1) * P, :])\
                        .then_inc(acc_in, 16)

            main = parts[2]
            for part in parts:
                if part is main:
                    with eng.Fori(0, B - 2) as b:
                        with eng.Fori(0, PAIRS - 1) as r:
                            loads(main, b * PAIRS + r + 1)
                        loads(main, b * PAIRS + PAIRS, closes=True)
                    with eng.Fori(0, PAIRS - 2) as r:
                        loads(main, r + (main.last - PAIRS + 2))
                    loads(main, main.last, more_x=False)
                else:
                    loads(part, part.first, closes=part.first == ITERS - PAIRS,
                          more_x=part.first < main.first)
            for o in range(KT):
                eng.wait_ge(fill_free, epilogue + 2 + 2 * o + 2)
                eng.dma_start(out[B - 1, o * P:(o + 1) * P, :], acc[:, o * T:(o + 1) * T])\
                    .then_inc(acc_out, 16)
            eng.wait_ge(acc_out, 16 * KT * B)

        @block.gpsimd
        def _(eng):
            eng.memset(minus_half[:, :], -0.5).then_inc(const_set, 1)
            eng.memset(p_shift[:, :], P_SHIFT).then_inc(const_set, 1)
            eng.memset(one_row[:, :], 1.0).then_inc(const_set, 1)
            for x in range(2):
                eng.memset(v_t[x][:, :], 1.0).then_inc(const_set, 1)
            eng.memset(p_bias[:, :], 0.0).then_inc(const_set, 1)

            def inverse_std(n, number):
                eng.wait_ge(fill_free, number + 1)
                wait(eng, y_done, n)
                eng.tensor_tensor(rstd[:, :], var_eps[:, :], minus_half[:, :], ALU.pow)\
                    .then_inc(rstd_done, 1)

            def norm_tile(n, batch, j, y):
                eng.wait_ge(xn_hi, n + 1)
                eng.tensor_tensor(xn_at(xn_l, batch, j, 0, T), y[:, :],
                                  xn_at(xn_h, batch, j, 0, T).bitcast(F32), ALU.subtract)\
                    .then_inc(xn_lo, 1)

            eng.wait_ge(const_set, 6 + CONST_DVE)
            for j in range(KT):
                inverse_std(j, number_of["var", j])
                norm_tile(j, 0, j, first_y(j))

            def low_parts(i, x, s):
                g = (2 * i + x) * NS + s
                eng.wait_ge(ph_done, g + 1)
                wait(eng, pv_done, g - 3)
                r = (s % 4) * T
                eng.tensor_tensor(p_l[:, r:r + T], p_f[:, r:r + T], p_h[:, r:r + T], ALU.subtract)\
                    .then_inc(pl_pool, 1)

            def body(part, i):
                if part.first < 0:
                    return
                for x in range(2):
                    for s in range(NS):
                        if x == 0 and s == 1 and part.xprep:
                            inverse_std(i + KT, part.number(i, ("var",), 0))
                        if s not in PL_ON_DVE:
                            low_parts(i, x, s)
                        if x == 0 and s == 4 and part.xprep:
                            norm_tile(i + KT, i // PAIRS + 1, i % PAIRS, xs)

            for_parts(eng, body)

        @block.scalar
        def _(eng):
            eng.wait_ge(const_set, 6 + CONST_DVE)
            for n in range(NW):
                u = number_of["wt", n]
                eng.wait_ge(fill_ready, u + 1)
                if n >= 2:
                    eng.wait_ge(w_stored[n % 2], 32 * (n // 2))
                ps = fill[u % 3]
                if n < NQK:
                    eng.activation(st_h[n % 2], ps[:, :], ACT.Copy, scale=QK_SCALE).then_inc(wt_hi, 1)
                elif n < NQK + NV:
                    eng.activation(st_h[n % 2], ps[:, :], ACT.Copy).then_inc(wt_hi, 1)
                else:
                    o = n - NQK - NV
                    if o == 0:
                        eng.wait_ge(w_steps, W_STEPS)
                    if o >= 1:
                        eng.wait_ge(fill_ready, number_of["pb", o - 1] + 1)
                    eng.activation(wt_f, ps[:, :], ACT.Copy).then_inc(wt_raw, 1)
                    for k in range(KT):
                        a = eng.activation(st_h[n % 2][:, k * P:(k + 1) * P], ps[:, k * P:(k + 1) * P],
                                           ACT.Copy, scale=v_inv[:, k:k + 1])
                    a.then_inc(wt_hi, 1)
                wait(eng, wt_hi, n + 1)
                wait(eng, fill_free, u + 1)
                for part, st in enumerate((st_h, st_l)):
                    if n < NQK:
                        dst = w_dram[n // 2, :, n % 2, part * C:(part + 1) * C]
                        src = st[n % 2].bitcast(F32)
                    elif n < NQK + NV:
                        dst = w_dram[n - NQK, :, 2, part * C:(part + 1) * C]
                        src = st[n % 2].bitcast(F32)
                    else:
                        c = part * C + (n - NQK - NV) * P
                        dst = w_dram[:, :, 3, c:c + P].rearrange("k p c -> p k c")
                        src = st[n % 2].bitcast(F32).rearrange("p (k c) -> p k c", k=KT)
                    eng.dma_start(dst, src).then_inc(w_stored[n % 2], 16)

            def norm_tile(n, batch, j, y):
                wait_apart(eng, y_done, n + 1)
                eng.activation(xn_at(xn_h, batch, j, 0, T), y[:, :], ACT.Copy).then_inc(xn_hi, 1)

            for j in range(KT):
                norm_tile(j, 0, j, first_y(j))

            def body(part, i):
                att = part.first >= 0
                for x in part.steps:
                    y = 1 - x
                    n = 2 * i + x
                    def high_parts(n, s):
                        g, r = n * NS + s, (s % 4) * T
                        eng.wait_ge(exp_done, g + 1)
                        wait(eng, pv_done, g - 3)
                        eng.activation(p_h[:, r:r + T], p_f[:, r:r + T], ACT.Copy).then_inc(ph_done, 1)

                    def second_k(half):
                        c = half * HALF
                        eng.wait_ge(qk_hi, 4 * (n + 1) + 2 * half + 2)
                        eng.activation(a_k[y][0:DH, c:c + HALF], a_k[y][DH:P, c:c + HALF].bitcast(F32),
                                       ACT.Copy).then_inc(k_copied, 1)

                    def of_unit(u):
                        ps = fill[part.bank(u, x)]
                        if u[0] in ("qk", "vt", "ot"):
                            wait_apart(eng, fill_ready, part.number(i, u, x) + 1)
                        if u[0] == "qk":
                            h, c = u[1], u[2] * HALF
                            head = (n + 1) % HEADS
                            for dst, to in ((a_q[h], 0), (a_k[h], DH)):
                                eng.activation(dst[to:to + DH, c:c + HALF], ps[to:to + DH, :],
                                               ACT.Identity,
                                               bias=qk_bias[to:to + DH, bass.ds(head, 1)])\
                                    .then_inc(qk_hi, 1)
                        elif u[0] == "vt":
                            eng.activation(v_cols(u[1], 0, DH),
                                           ps[:, :].rearrange("p (s d) -> p s d", s=NS), ACT.Copy)\
                                .then_inc(vt_hi, 1)
                        elif u[0] == "ot":
                            c = u[1] * HALF
                            eng.activation(at_h[:, c:c + HALF], ps[:, :], ACT.Copy).then_inc(at_hi, 1)

                    for s in range(NS):
                        units = part.slots[x][s]
                        if s == 1 and ("qk", y, 1) in units:
                            of_unit(("qk", y, 1))
                        if att:
                            g = n * NS + s
                            r = (s % 4) * T
                            eng.wait_ge(logits_ready, g + 1)
                            wait(eng, exp_done, g - 3)
                            wait(eng, ph_done, g - 3)
                            wait_low(eng, n, s)
                            eng.activation(p_f[:, r:r + T], logits[:, :], ACT.Exp, bias=p_shift[:, :])\
                                .then_inc(exp_done, 1)
                        if s == 1 and (att and not (x == 0 and part.first == 0)):
                            eng.wait_ge(pv_done, n * NS)
                            wait(eng, o_sum_done, n - 1)
                            eng.wait_ge(r_done, n)
                            eng.activation(nine(o_low), o_tiles(DH + 1, 2 * DH + 1), ACT.Copy)\
                                .then_inc(o_low_done, 1)
                        for u in units:
                            if u[0] in ("vt", "ot"):
                                of_unit(u)
                        if s == 1 and ("qk", y, 1) in units:
                            second_k(1)
                        if att:
                            high_parts(n, s)
                        if s == 2 and ("qk", y, 1) in part.slots[x][1]:
                            eng.wait_ge(qk_hi, 4 * (n + 1) + 4)
                            eng.dma_start(b_q[y][0:DH, :].bitcast(F32), a_q[y][0:DH, :].bitcast(F32))\
                                .then_inc(dup_q[y], 16)
                        if s == 0 and ("qk", y, 0) in units:
                            of_unit(("qk", y, 0))
                            second_k(0)
                        if x == 0 and s == 3 and part.xprep:
                            norm_tile(i + KT, i // PAIRS + 1, i % PAIRS, xs)

            for_parts(eng, body)
            last = 2 * ITERS
            eng.wait_ge(pv_done, last * NS)
            eng.wait_ge(o_sum_done, last - 1)
            eng.wait_ge(r_done, last)
            eng.activation(nine(o_low), o_tiles(DH + 1, 2 * DH + 1), ACT.Copy).then_inc(o_low_done, 1)
            for h in range(2):
                u = epilogue + h
                eng.wait_ge(fill_ready, u + 1)
                eng.activation(at_h[:, h * HALF:(h + 1) * HALF], fill[u % 3][:, :], ACT.Copy)\
                    .then_inc(at_hi, 1)

        @block.vector
        def _(eng):
            eng.memset(o_ps[:, :], 1.0).then_inc(const_set, 1)
            eng.wait_ge(const_set, 6 + 1)
            for x in range(2):
                for u in range(2):
                    eng.tensor_copy(b_k[x][DH:DH + NS, u * HALF:(u + 1) * HALF], one_row[DH:DH + NS, :])\
                        .then_inc(const_set, 1)

            eng.wait_ge(const_loaded, 16 * CONST_LOADS)
            count = 0

            def step(a):
                nonlocal count
                count += 1
                a.then_inc(w_steps, 1)
                eng.wait_ge(w_steps, count)

            def scale_tile(n):
                w = raw[n % 2]
                if n < NQK + NV:
                    eng.wait_ge(w_loaded[n % 2], W_SEEN[n])
                    if n >= 2:
                        eng.wait_ge(fill_ready, number_of["wt", n - 2] + 1)
                    step(eng.tensor_tensor_reduce(out=waste, in0=w, in1=beta, scale=1.0, scalar=0.0,
                                                  op0=ALU.mult, op1=ALU.add, accum_out=dots[:, n:n + 1]))
                    m = eng.tensor_tensor(scaled[n % 2], w, gamma, ALU.mult)
                    if n < NQK:
                        m.then_inc(w_scaled, 1)
                        step(eng.tensor_scalar(qk_bias[:, n:n + 1], dots[:, n:n + 1], b_cols[:, n:n + 1],
                                               QK_SCALE, ALU.add, ALU.mult))
                    else:
                        p = n - NQK
                        step(m)
                        step(eng.tensor_reduce(v_inv[:, p:p + 1], scaled[n % 2], AX.X, ALU.add,
                                               apply_absolute_value=True))
                        step(eng.tensor_scalar(v_inv[:, p:p + 1], v_inv[:, p:p + 1],
                                               XN_MAX / V_RANGE, 1e-30, ALU.mult, ALU.max))
                        step(eng.reciprocal(v_scl[:, p:p + 1], v_inv[:, p:p + 1]))
                        step(eng.tensor_scalar(v_bias[:, p:p + 1], dots[:, n:n + 1], b_cols[:, n:n + 1],
                                               None, ALU.add))
                        eng.tensor_scalar(scaled[n % 2], scaled[n % 2], v_scl[:, p:p + 1],
                                          None, ALU.mult).then_inc(w_scaled, 1)

            def low_tile(n):
                u = number_of["wt", n]
                ps = fill[u % 3]
                eng.wait_ge(wt_hi, n + 1)
                if n >= 2:
                    eng.wait_ge(w_stored[n % 2], 32 * (n // 2))
                if n < NQK:
                    eng.scalar_tensor_tensor(st_l[n % 2], ps[:, :], QK_SCALE, st_h[n % 2].bitcast(F32),
                                             ALU.mult, ALU.subtract).then_inc(fill_free, 1)
                elif n < NQK + NV:
                    eng.tensor_tensor(st_l[n % 2], ps[:, :], st_h[n % 2].bitcast(F32), ALU.subtract)\
                        .then_inc(fill_free, 1)
                else:
                    for k in range(KT):
                        a = eng.scalar_tensor_tensor(st_l[n % 2][:, k * P:(k + 1) * P],
                                                     ps[:, k * P:(k + 1) * P], v_inv[:, k:k + 1],
                                                     st_h[n % 2][:, k * P:(k + 1) * P].bitcast(F32),
                                                     ALU.mult, ALU.subtract)
                    a.then_inc(fill_free, 1)
                    o = n - NQK - NV
                    u = number_of["pb", o]
                    eng.wait_ge(fill_ready, u + 1)
                    eng.tensor_scalar(p_bias[:, o:o + 1], fill[u % 3][:, 0:1], b_cols[:, n:n + 1],
                                      None, ALU.add).then_inc(fill_free, 1)

            scale_tile(0)
            for n in range(NW):
                if n + 1 < NW:
                    scale_tile(n + 1)
                low_tile(n)

            def stats(n, x):
                for h in range(2):
                    a = eng.bn_stats(bn[:, 6 * h:6 * h + 6], x[:, h * HALF:(h + 1) * HALF])
                a.then_inc(bn_done, 1)
                wait_apart(eng, bn_done, 2 * n + 1)
                eng.bn_aggr(mv[:, :], bn[:, :]).then_inc(bn_done, 1)

            def mean_unit(n, number, bank):
                eng.wait_ge(fill_ready, number + 1)
                eng.tensor_copy(g_mean[:, :], fill[bank][:, 0:1]).then_inc(fill_free, 1)
                eng.wait_ge(fill_free, number + 1)
                eng.tensor_tensor(dev[:, :], mv[:, 0:1], g_mean[:, :], ALU.subtract).then_inc(x_steps, 1)
                eng.wait_ge(x_steps, 3 * n + 1)
                eng.tensor_tensor(var_in[:, :], dev[:, :], dev[:, :], ALU.mult).then_inc(x_steps, 1)
                eng.wait_ge(x_steps, 3 * n + 2)
                eng.tensor_tensor(var_in[:, :], var_in[:, :], mv[:, 1:2], ALU.add).then_inc(x_steps, 1)

            def var_unit(n, number, bank):
                eng.wait_ge(fill_ready, number + 1)
                eng.tensor_scalar(var_eps[:, :], fill[bank][:, 0:1], EPS, None, ALU.add)\
                    .then_inc(fill_free, 1)

            def normalise(n, y, x):
                eng.wait_ge(rstd_done, n + 1)
                eng.tensor_scalar(y[:, :], x, g_mean[:, 0:1], rstd[:, 0:1],
                                  ALU.subtract, ALU.mult).then_inc(y_done, 1)

            eng.wait_ge(acc_in, 16 * KT)
            x0 = [acc[:, j * T:(j + 1) * T] for j in range(KT)]
            stats(0, x0[0])
            for j in range(KT):
                mean_unit(j, number_of["mean", j], number_of["mean", j] % 3)
                var_unit(j, number_of["var", j], number_of["var", j] % 3)
                if j + 1 < KT:
                    stats(j + 1, x0[j + 1])
                if j >= 2:
                    eng.wait_ge(xn_lo, j - 1)
                normalise(j, first_y(j), x0[j])
                eng.wait_ge(y_done, j + 1)

            def low_parts(n, s):
                g = n * NS + s
                eng.wait_ge(ph_done, g + 1)
                wait(eng, pv_done, g - 3)
                r = (s % 4) * T
                eng.tensor_tensor(p_l[:, r:r + T], p_f[:, r:r + T], p_h[:, r:r + T], ALU.subtract)\
                    .then_inc(pl_dve, 1)

            def row_sums(n):
                eng.wait_ge(pv_done, (n + 1) * NS)
                wait(eng, o_n_done, n)
                eng.reciprocal(r_sum[:, :].rearrange("p (g t a) -> p g t a", g=3, a=1),
                               o_tiles(DH, DH + 1)).then_inc(r_done, 1)

            def output(n):
                eng.wait_ge(o_low_done, n + 1)
                eng.tensor_tensor(nine(o_sum), o_tiles(0, DH), nine(o_low), ALU.add)\
                    .then_inc(o_sum_done, 1)

            def normed(n, x):
                eng.wait_ge(o_sum_done, n + 1)
                eng.wait_ge(r_done, n + 1)
                dst = o_n[:, :].rearrange("p (t c) -> p t c", t=NS)[:, :, x * DH:(x + 1) * DH]
                src = o_sum[:, 0:NS * DH].rearrange("p (t d) -> p t d", t=NS)
                rs = r_sum[:, 0:NS].rearrange("p (t a) -> p t a", a=1).to_broadcast([P, NS, DH])
                eng.tensor_tensor(dst, src, rs, ALU.mult).then_inc(o_n_done, 1)

            def attention_sum(u, number, bank, i, b):
                o, h = u[1] // 2, u[1] % 2
                eng.wait_ge(fill_ready, number + 1)
                if u[1] == 0:
                    eng.wait_ge(acc_in, 16 * KT * (b + 1))
                c = o * T + h * HALF
                p = (i - 1) % PAIRS
                eng.scalar_tensor_tensor(acc[:, c:c + HALF], fill[bank][:, :],
                                         p_bias[:, bass.ds(p * KT + o, 1)], acc[:, c:c + HALF],
                                         ALU.add, ALU.add).then_inc(fill_free, 1)

            def unit(part, i, x, u):
                n = 2 * i + x
                number, bank = part.number(i, u, x), part.bank(u, x)
                ps = fill[bank]
                if u[0] == "qk":
                    h, half = u[1], u[2]
                    c = half * HALF
                    head = (n + 1) % HEADS
                    eng.wait_ge(qk_hi, 4 * (n + 1) + 2 * half + 1)
                    eng.scalar_tensor_tensor(a_q[h][DH:P, c:c + HALF], ps[0:DH, :],
                                             qk_bias[0:DH, bass.ds(head, 1)],
                                             a_q[h][0:DH, c:c + HALF].bitcast(F32), ALU.add, ALU.subtract)\
                        .then_inc(q_lo, 1)
                    eng.wait_ge(qk_hi, 4 * (n + 1) + 2 * half + 2)
                    eng.scalar_tensor_tensor(b_k[h][0:DH, c:c + HALF], ps[DH:P, :],
                                             qk_bias[DH:P, bass.ds(head, 1)],
                                             a_k[h][DH:P, c:c + HALF].bitcast(F32), ALU.add, ALU.subtract)\
                        .then_inc(fill_free, 1)
                elif u[0] == "max":
                    _, h, tt, half = u
                    eng.wait_ge(fill_ready, number + 1)
                    if (tt, half) == MAX_ORDER[0]:
                        wait(eng, neg_done, n + 1)
                    eng.tensor_reduce(row_max[:, 2 * tt + half:2 * tt + half + 1], ps[:, :], AX.X, ALU.max)\
                        .then_inc(fill_free, 1)
                    if (tt, half) == MAX_ORDER[-1]:
                        eng.wait_ge(fill_free, number + 1)
                        eng.tensor_reduce(neg_max[:, :], row_max[:, :].rearrange("p (t h) -> p t h", h=2),
                                          AX.X, ALU.max, negate=True).then_inc(neg_done, 1)
                elif u[0] == "m":
                    h = u[1]
                    eng.wait_ge(fill_ready, number + 1)
                    src = ps[0:NS, 0:P].rearrange("j (a c) -> j a c", a=1).to_broadcast([NS, NS, P])
                    eng.tensor_tensor(b_q[h][DH:DH + NS, :].rearrange("j (a c) -> j a c", a=NS), src,
                                      own_tile[:, :].rearrange("j (a c) -> j a c", a=NS), ALU.mult)\
                        .then_inc(fill_free, 1)
                elif u[0] == "v":
                    eng.wait_ge(fill_ready, number + 1)
                    eng.tensor_copy(v_f[:, u[1] * HALF:(u[1] + 1) * HALF], ps[:, :]).then_inc(fill_free, 1)
                elif u[0] == "vt":
                    h = u[1]
                    eng.wait_ge(vt_hi, n + 2)
                    eng.tensor_tensor(v_cols(h, DH + 1, 2 * DH + 1),
                                      ps[:, :].rearrange("p (s d) -> p s d", s=NS),
                                      v_cols(h, 0, DH), ALU.subtract).then_inc(fill_free, 1)
                elif u[0] == "ot":
                    c = u[1] * HALF
                    eng.wait_ge(at_hi, 2 * (i - 1) + u[1] + 1)
                    eng.tensor_tensor(at_l[:, c:c + HALF], ps[:, :], at_h[:, c:c + HALF].bitcast(F32),
                                      ALU.subtract).then_inc(fill_free, 1)
                elif u[0] == "proj":
                    attention_sum(u, number, bank, i, (i - 1) // PAIRS)
                elif u[0] == "mean":
                    mean_unit(i + KT, number, bank)
                elif u[0] == "var":
                    var_unit(i + KT, number, bank)

            def body(part, i):
                att = part.first >= 0
                for x in part.steps:
                    n = 2 * i + x
                    for s in range(NS):
                        first_step = part.first == 0 and x == 0
                        if x == 0 and s == 0 and part.xprep:
                            eng.wait_ge(xs_in, 16 * (i + 1))
                            stats(i + KT, xs)
                        units = part.slots[x][s]
                        if s == 6:
                            for u in units[:1]:
                                unit(part, i, x, u)
                            units = units[1:]
                        if att and s - 1 in PL_ON_DVE:
                            low_parts(n, s - 1)
                        if s == 1 and ("qk", 1 - x, 1) in units:
                            unit(part, i, x, units[0])
                            units = units[1:]
                        if units[:1] == [("var",)]:
                            unit(part, i, x, units[0])
                            units = units[1:]
                        if s == 1 and att and not first_step:
                            row_sums(n - 1)
                            if units:
                                unit(part, i, x, units[0])
                                units = units[1:]
                            output(n - 1)
                        for u in units:
                            unit(part, i, x, u)
                        if s == 1 and att and not first_step:
                            normed(n - 1, 1 - x)
                        if x == 0 and s == 2 and part.xprep:
                            normalise(i + KT, xs, xs[:, :])

            for_parts(eng, body)
            last = 2 * ITERS
            row_sums(last - 1)
            output(last - 1)
            normed(last - 1, 1)
            for h in range(2):
                u = epilogue + h
                c = h * HALF
                eng.wait_ge(at_hi, 2 * (ITERS - 1) + h + 1)
                eng.tensor_tensor(at_l[:, c:c + HALF], fill[u % 3][:, :], at_h[:, c:c + HALF].bitcast(F32),
                                  ALU.subtract).then_inc(fill_free, 1)
            for k in range(2 * KT):
                u = epilogue + 2 + k
                attention_sum(("proj", k), u, u % 3, ITERS, B - 1)

        @block.tensor
        def _(eng):
            def bank_free(number):
                wait(eng, fill_free, number - 2)

            eng.wait_ge(const_loaded, 16 * CONST_LOADS)
            eng.wait_ge(const_set, 6 + CONST_DVE)
            for n in range(NW):
                u = number_of["wt", n]
                bank_free(u)
                if n < NQK + NV:
                    eng.wait_ge(w_scaled, n + 1)
                    src = scaled[n % 2]
                else:
                    eng.wait_ge(w_loaded[n % 2], W_SEEN[n])
                    src = raw[n % 2]
                for k in range(KT):
                    a = eng.transpose(fill[u % 3][:, k * P:(k + 1) * P], src[:, k * P:(k + 1) * P],
                                      ident[:, :])
                a.then_inc(fill_ready, 1)
                if n >= NQK + NV:
                    o = n - NQK - NV
                    u = number_of["pb", o]
                    bank_free(u)
                    eng.wait_ge(wt_raw, o + 1)
                    eng.wait_ge(w_steps, W_STEPS)
                    for k in range(KT):
                        a = eng.matmul(fill[u % 3][:, 0:1], wt_f[:, k * P:(k + 1) * P],
                                       v_bias[:, k:k + 1], start=k == 0, stop=k == KT - 1)
                    a.then_inc(fill_ready, 1)

            def mean_unit(n, number, bank):
                bank_free(number)
                eng.wait_ge(bn_done, 2 * n + 2)
                eng.matmul(fill[bank][:, 0:1], group_mean[:, :], mv[:, 0:1], start=True, stop=True)\
                    .then_inc(fill_ready, 1)

            def var_unit(n, number, bank):
                bank_free(number)
                eng.wait_ge(x_steps, 3 * n + 3)
                eng.matmul(fill[bank][:, 0:1], group_mean[:, :], var_in[:, :], start=True, stop=True)\
                    .then_inc(fill_ready, 1)

            for j in range(KT):
                mean_unit(j, number_of["mean", j], number_of["mean", j] % 3)
                var_unit(j, number_of["var", j], number_of["var", j] % 3)

            def project(ps, w, batch, half, third):
                products = [(k, wp, xp) for k in range(KT) for wp, xp in ((0, xn_h), (0, xn_l), (1, xn_h))]
                n = len(products)
                for m in range(third * n // 3, (third + 1) * n // 3):
                    k, wp, xp = products[m]
                    c = wp * C + k * P
                    a = eng.matmul(ps[:, :], w[:, c:c + P], xn_at(xp, batch, k, half * HALF, HALF),
                                   start=m == 0, stop=m == n - 1)
                return a

            def out_product(u, bank):
                o, h = u[1] // 2, u[1] % 2
                c = h * HALF
                for m, (wp, ap) in enumerate(((0, at_h), (0, at_l), (1, at_h))):
                    a = eng.matmul(fill[bank][:, :], w_p[:, wp * C + o * P:wp * C + (o + 1) * P],
                                   ap[:, c:c + HALF], start=m == 0, stop=m == 2)
                a.then_inc(fill_ready, 1)

            def turn_output(u, bank):
                for k in range(4):
                    tt = 4 * u[1] + k
                    a = eng.transpose(fill[bank][:, k * P:(k + 1) * P], o_n[:, tt * P:(tt + 1) * P],
                                      ident[:, :])
                a.then_inc(fill_ready, 1)

            def unit(part, i, x, u):
                number, bank = part.number(i, u, x), part.bank(u, x)
                n = 2 * i + x
                ps = fill[bank]
                if u[0] == "mean":
                    return mean_unit(i + KT, number, bank)
                if u[0] == "var":
                    return var_unit(i + KT, number, bank)
                after = {("vt", 0): ("v", 1), ("proj", 0): ("ot", 1)}.get(u)
                due = part.index[u, x] - 2
                if after is not None:
                    due = max(due, part.index[after, x] + 1)
                (wait_apart if u[0] == "vt" else wait)(eng, fill_free, part.start(i) + due)
                if u[0] == "vt":
                    h = u[1]
                    r = h * DH
                    for s in range(NS):
                        a = eng.transpose(ps[:, s * DH:(s + 1) * DH], v_f[r:r + DH, s * P:(s + 1) * P],
                                          ident[r:r + DH, r:r + DH])
                    a.then_inc(fill_ready, 1)
                elif u[0] == "max":
                    _, y, tt, half = u
                    if (tt, half) == MAX_ORDER[0]:
                        eng.wait_ge(q_lo, 2 * (n + 1) + 1)
                        eng.wait_ge(k_copied, 2 * (n + 1) + 1)
                    if (tt, half) == MAX_ORDER[len(MAX_EARLY)]:
                        eng.wait_ge(q_lo, 2 * (n + 1) + 2)
                        eng.wait_ge(k_copied, 2 * (n + 1) + 2)
                    eng.matmul(ps[:, :], a_q[y][:, tt * P:(tt + 1) * P],
                               a_k[y][:, half * HALF:(half + 1) * HALF], start=True, stop=True)\
                        .then_inc(fill_ready, 1)
                elif u[0] == "m":
                    eng.wait_ge(neg_done, n + 2)
                    eng.transpose(ps[0:NS, 0:P], neg_max[:, :], ident[:, :]).then_inc(fill_ready, 1)
                elif u[0] == "ot":
                    if u[1] == 0:
                        eng.wait_ge(o_n_done, 2 * i)
                    turn_output(u, bank)
                elif u[0] == "proj":
                    if u[1] == 0:
                        eng.wait_ge(wp_in, 16 * i)
                    out_product(u, bank)

            def pieces_of(units):
                out = [(u, None) for u in units]
                for k, u in enumerate(units):
                    if u[0] in ("qk", "v"):
                        out[k] = (u, 2)
                        out.insert(max(0, k - 1), (u, 1))
                        out.insert(max(0, k - 2), (u, 0))
                        break
                return out

            def piece(part, i, x, u, third):
                if third is None:
                    unit(part, i, x, u)
                    return
                ps = fill[part.bank(u, x)]
                if u[0] == "qk":
                    w, pair, half, loaded = w_qk[u[1]], i + x, u[2], wqk_in[u[1]]
                else:
                    w, pair, half, loaded = w_v, i + 1, u[1], wv_in
                if third == 0:
                    wait(eng, fill_free, part.start(i) + part.index[u, x] - 2)
                    if half == 0:
                        eng.wait_ge(loaded, 16 * (pair + 1))
                        if u[:2] == ("qk", 0):
                            eng.wait_ge(xn_lo, KT * (pair // PAIRS) + KT)
                a = project(ps, w, pair // PAIRS, half, third)
                if third == 2:
                    a.then_inc(fill_ready, 1)

            def scores(part, i, x, s):
                n = 2 * i + x
                g = n * NS + s
                if s == 0:
                    if x == 1:
                        eng.wait_ge(fill_free, part.number(i, ("m", 1), 0) + 1)
                    else:
                        eng.wait_ge(fill_free, part.start(i))
                    eng.wait_ge(dup_q[x], 16 * (i + 1))
                wait(eng, exp_done, g)
                for h in range(2):
                    c = h * HALF
                    eng.matmul(logits[:, c:c + HALF], a_k[x][:, s * P:(s + 1) * P], a_q[x][:, c:c + HALF],
                               start=True, stop=False)
                    a = eng.matmul(logits[:, c:c + HALF], b_k[x][0:DH + NS, s * P:(s + 1) * P],
                                   b_q[x][0:DH + NS, c:c + HALF], start=False, stop=True)
                a.then_inc(logits_ready, 1)

            def values(n, x, s, first, end):
                g = n * NS + s
                if first == 0:
                    if s == 0:
                        wait(eng, o_sum_done, n)
                    wait_low_of(eng, n, s)
                r = (s % 4) * T
                v = v_t[x]
                for tt in range(first, end):
                    c = r + tt * P
                    eng.matmul(o_tile(tt, 0, DH + 1), p_l[:, c:c + P], v[:, s * VW:s * VW + DH + 1],
                               start=s == 0 and tt % OT_BANK == 0, stop=False, skip_group_check=True)
                    a = eng.matmul(o_tile(tt, 0, 2 * DH + 1), p_h[:, c:c + P], v[:, s * VW:s * VW + 2 * DH + 1],
                                   start=False, stop=s == NS - 1, skip_group_check=True)
                if end == NS:
                    a.then_inc(pv_done, 1)

            def body(part, i):
                att = part.first >= 0
                for x in part.steps:
                    n = 2 * i + x
                    for s in range(NS):
                        units = pieces_of(part.slots[x][s])
                        if not att:
                            for u in units:
                                piece(part, i, x, *u)
                            continue
                        pn, px, ps = (n, x, s - 2) if s >= 2 else (n - 1, 1 - x, NS - 2 + s)
                        has_values = not (part.first == 0 and x == 0 and s < 2)
                        done = 0 if has_values else NS
                        if s == 0 and has_values:
                            values(pn, px, ps, 0, NS)
                            done = NS
                        if s == 1:
                            for u in [u for u in units if u[0][0] in ("qk", "var")]:
                                piece(part, i, x, *u)
                            units = [u for u in units if u[0][0] not in ("qk", "var")]
                        scores(part, i, x, s)
                        if s == 1 and has_values:
                            values(pn, px, ps, 0, NS)
                            done = NS
                        if s == NS - 1:
                            done = NS // 2 + 1
                            values(pn, px, ps, 0, done)
                        for k, u in enumerate(units):
                            piece(part, i, x, *u)
                            upto = (k + 1) * NS // len(units)
                            if upto > done and not (s == 2 and k == 0):
                                values(pn, px, ps, done, upto)
                                done = upto
                        if done < NS:
                            values(pn, px, ps, done, NS)

            for_parts(eng, body)
            last = 2 * ITERS
            values(last - 1, 1, NS - 2, 0, NS)
            values(last - 1, 1, NS - 1, 0, NS)
            eng.wait_ge(o_n_done, last)
            for h in range(2):
                bank_free(epilogue + h)
                turn_output(("ot", h), (epilogue + h) % 3)
            eng.wait_ge(wp_in, 16 * ITERS)
            eng.wait_ge(fill_free, epilogue + 2)
            for k in range(2 * KT):
                u = epilogue + 2 + k
                bank_free(u)
                out_product(("proj", k), u % 3)


CONST_DVE = 1 + 4
_LOADS = [1] * HEADS + [2] * PAIRS + [1] * KT
W_SEEN = [16 * sum(_LOADS[m] for m in range(n % 2, n + 1, 2)) for n in range(len(_LOADS))]
W_STEPS = 2 * HEADS + 6 * PAIRS


def kernel(x, L0_conv_gn_scale, L0_conv_gn_bias, L0_conv_w_qkv, L0_conv_b_qkv, L0_conv_w_proj,
           L0_conv_b_proj):
    import numpy as np
    from concourse import bacc
    from concourse.bass_utils import run_bass_kernel_spmd

    nc = bacc.Bacc("TRN2", target_bir_lowering=False, num_devices=1)
    ch = np.arange(P)
    per_group = C // GROUPS
    group = (ch[:, None] // per_group == ch[None, :] // per_group).astype(np.float32) / per_group
    mask = (np.arange(T)[None, :] // P == np.arange(NS)[:, None]).astype(np.float32)
    arrays = {
        "x": np.ascontiguousarray(x).reshape(B, C, T),
        "gn_scale": np.ascontiguousarray(L0_conv_gn_scale),
        "gn_bias": np.ascontiguousarray(L0_conv_gn_bias),
        "w_qkv": np.ascontiguousarray(L0_conv_w_qkv),
        "b_qkv": np.ascontiguousarray(L0_conv_b_qkv),
        "w_proj": np.ascontiguousarray(L0_conv_w_proj),
        "b_proj": np.ascontiguousarray(L0_conv_b_proj),
        "ident": np.eye(P, dtype=np.float32),
        "group_mean": group,
        "own_tile": mask,
    }
    arrays = {f"in_{k}": a for k, a in arrays.items()}
    args = [nc.dram_tensor(k, a.shape, F32, kind="ExternalInput").ap() for k, a in arrays.items()]
    out = nc.dram_tensor("out", (B, C, T), F32, kind="ExternalOutput").ap()
    w_dram = nc.dram_tensor("w_dram", (PAIRS, P, 4, 2 * C), F32, kind="Internal").ap()
    attention_block(nc, *args, out, w_dram)
    r = run_bass_kernel_spmd(nc, [arrays], core_ids=[0])
    return r.results[0]["out"].reshape(B, C, 32, 32)
```
